# Optimizing a Trainium2 kernel written in Bass

```python
import numpy as np
import jax
import jax.numpy as jnp

def _softmax(x, axis=-1):
    return jax.nn.softmax(x, axis=axis)

def _gelu(x):
    return jax.nn.gelu(x, approximate=True)

def _silu(x):
    return jax.nn.silu(x)

def _sigmoid(x):
    return jax.nn.sigmoid(x)

def _layernorm(x, axis=-1, eps=1e-05):
    m = jnp.mean(x, axis=axis, keepdims=True)
    v = jnp.var(x, axis=axis, keepdims=True)
    return (x - m) / jnp.sqrt(v + eps)

def _scatter_add(tgt, idx, src, axis=0):
    return tgt.at[idx].add(src)

def _segment_sum(src, seg, n):
    return jax.ops.segment_sum(src, seg, n)
kernel_name = 'mk_xattn_ffn_d2_seqx_r8_5f4de2'

def setup_inputs(seed: int=0):
    np.random.seed(seed)
    _w = jnp.asarray

    def _rec_inputs():
        import jax
        import jax.numpy as jnp
        _rk = jax.random.key(seed)
        x = 7.22e-05 + 1 * jax.random.normal(jax.random.fold_in(_rk, 1), (4, 512, 128), jnp.float32)
        _lenS = 512 - jax.random.randint(jax.random.fold_in(_rk, 7), (4,), 0, max(1, 512 // 4) + 1, jnp.int32)
        _lenS2 = 77 - jax.random.randint(jax.random.fold_in(_rk, 8), (4,), 0, max(1, 77 // 4) + 1, jnp.int32)
        _ctx_1024P = jax.random.normal(jax.random.fold_in(_rk, 11), (4, 16, 128), jnp.float32)
        _ctx_1024c = jax.random.dirichlet(jax.random.fold_in(_rk, 511), 0.3 * jnp.ones((16,), jnp.float32), (4, 77))
        _ctx_1024t = jnp.einsum('bsk,bkd->bsd', _ctx_1024c, _ctx_1024P)
        _ctx_1024t = _ctx_1024t * jax.lax.rsqrt(jnp.mean(jnp.square(_ctx_1024t)) + 1e-12) * 0.953939
        ctx_1024 = -0.000514642 + 1.00011 * (_ctx_1024t + 0.3 * jax.random.normal(jax.random.fold_in(_rk, 611), (4, 77, 128), jnp.float32))
        return (x, ctx_1024)
    x, ctx_1024 = _rec_inputs()

    def _L0_xattn_setup():
        import jax, jax.numpy as jnp
        import numpy as np
        B, L_ENC, L_DEC, D = (16, 64, 128, 128)
        key = jax.random.key(seed)
        k1, k2, k3, k4, k5, k6 = jax.random.split(key, 6)
        encoder_hc = jax.random.normal(k1, (B, L_ENC, D), dtype=jnp.float32)
        decoder_hq = jax.random.normal(k2, (B, L_DEC, D), dtype=jnp.float32)
        w_sim = jax.random.normal(k3, (3 * D,), dtype=jnp.float32) * 0.02
        b_sim = jax.random.normal(k4, (1,), dtype=jnp.float32) * 0.02
        W_qv = jax.random.normal(k5, (4 * D, D), dtype=jnp.float32) * 0.02
        b_qv = jax.random.normal(k6, (D,), dtype=jnp.float32) * 0.02
        return {'encoder_hc': encoder_hc, 'decoder_hq': decoder_hq, 'w_sim': w_sim, 'b_sim': b_sim, 'W_qv': W_qv, 'b_qv': b_qv}
    _L0_xattn_all = _L0_xattn_setup()
    _L0_xattn_in = {k: v for k, v in _L0_xattn_all.items() if k in ('w_sim', 'b_sim', 'W_qv', 'b_qv')}
    del _L0_xattn_all

    def _L0_ffn_setup():
        import jax, jax.numpy as jnp
        import numpy as np
        DIM = 128
        DEPTH = 6
        HEADS = 16
        DIM_HEAD = 64
        WINDOW = 32
        INNER = HEADS * DIM_HEAD
        DIM_INNER = int(DIM * 4 * 2 / 3)
        QK_SCALE = 8.0

        def shift_tokens(t):
            a, s = jnp.split(t, 2, -1)
            s = jnp.pad(s, ((0, 0), (1, 0), (0, 0)))[:, :-1]
            return jnp.concatenate([a, s], -1)

        def l2norm(t):
            return t / jnp.maximum(jnp.linalg.norm(t, axis=-1, keepdims=True), 1e-12)

        def rotate_half(x):
            x1, x2 = jnp.split(x, 2, -1)
            return jnp.concatenate([-x2, x1], -1)

        def rotary_tables(n):
            half = jnp.arange(0, DIM_HEAD, 2, dtype=jnp.float32)
            inv_freq = 1.0 / 10000.0 ** (half / DIM_HEAD)
            t = jnp.arange(n, dtype=jnp.float32)
            freqs = t[:, None] * inv_freq[None, :]
            freqs = jnp.concatenate([freqs, freqs], -1)
            base_scale = (half + 0.4 * DIM_HEAD) / (1.4 * DIM_HEAD)
            power = (t - n // 2) / (WINDOW // 2)
            scale = base_scale[None, :] ** power[:, None]
            scale = jnp.concatenate([scale, scale], -1)
            return (freqs, scale)

        def local_attention(q, k, v):
            b, h, n, d = q.shape
            w = WINDOW
            nw = n // w
            bq = q.reshape(b, h, nw, w, d)
            bk = k.reshape(b, h, nw, w, d)
            bv = v.reshape(b, h, nw, w, d)

            def look(t):
                p = jnp.pad(t, ((0, 0), (0, 0), (1, 0), (0, 0), (0, 0)))
                return jnp.concatenate([p[:, :, :nw], p[:, :, 1:]], axis=3)
            bk2, bv2 = (look(bk), look(bv))
            seq = jnp.arange(n).reshape(nw, w)
            seq_p = jnp.pad(seq, ((1, 0), (0, 0)), constant_values=-1)
            jt = jnp.concatenate([seq_p[:nw], seq_p[1:]], axis=1)
            it = seq[:, :, None]
            jb = jt[:, None, :]
            mask = (it < jb) | (it > jb + w) | (jb == -1)
            sim = jnp.einsum('bhwie,bhwje->bhwij', bq, bk2) * QK_SCALE
            sim = jnp.where(mask, -jnp.finfo(sim.dtype).max, sim)
            attn = jax.nn.softmax(sim, -1)
            out = jnp.einsum('bhwij,bhwje->bhwie', attn, bv2)
            return out.reshape(b, h, n, d)

        def attn_layer(x, Wqkv, qs, ksc, Wo):
            b, n, _ = x.shape
            qkv = x @ Wqkv
            q, k, v = jnp.split(qkv, 3, -1)
            sh = lambda t: t.reshape(b, n, HEADS, DIM_HEAD).transpose(0, 2, 1, 3)
            q, k, v = (sh(q), sh(k), sh(v))
            q = l2norm(q) * qs
            k = l2norm(k) * ksc
            freqs, scale = rotary_tables(n)
            cos, sin = (jnp.cos(freqs), jnp.sin(freqs))
            q = q * cos * scale + rotate_half(q) * sin * scale
            inv = 1.0 / scale
            k = k * cos * inv + rotate_half(k) * sin * inv
            out = local_attention(q, k, v)
            out = out.transpose(0, 2, 1, 3).reshape(b, n, INNER)
            return out @ Wo

        def ffn_layer(x, g, bln, W1, b1, W2, b2):
            mu = x.mean(-1, keepdims=True)
            var = ((x - mu) ** 2).mean(-1, keepdims=True)
            xn = (x - mu) / jnp.sqrt(var + 1e-05) * g + bln
            hg = xn @ W1 + b1
            a, gate = jnp.split(hg, 2, -1)
            return a * jax.nn.gelu(gate, approximate=False) @ W2 + b2
        key = jax.random.key(seed)
        ks = jax.random.split(key, 8)
        B, N = (2, 256)
        init = lambda k, shape: jax.random.normal(k, shape, jnp.float32) * 0.02
        return {'x': jax.random.normal(ks[0], (B, N, DIM), jnp.float32), 'Wqkv': init(ks[1], (DEPTH, DIM, 3 * INNER)), 'q_scale': jnp.ones((DEPTH, DIM_HEAD), jnp.float32), 'k_scale': jnp.ones((DEPTH, DIM_HEAD), jnp.float32), 'Wo': init(ks[2], (DEPTH, INNER, DIM)), 'ln_g': jnp.ones((DEPTH, DIM), jnp.float32), 'ln_b': jnp.zeros((DEPTH, DIM), jnp.float32), 'W1': init(ks[3], (DEPTH, DIM, 2 * DIM_INNER)), 'b1': jnp.zeros((DEPTH, 2 * DIM_INNER), jnp.float32), 'W2': init(ks[4], (DEPTH, DIM_INNER, DIM)), 'b2': jnp.zeros((DEPTH, DIM), jnp.float32)}
    _L0_ffn_all = _L0_ffn_setup()
    _L0_ffn_in = {k: v for k, v in _L0_ffn_all.items() if k in ('Wqkv', 'q_scale', 'k_scale', 'Wo', 'ln_g', 'ln_b', 'W1', 'b1', 'W2', 'b2')}
    del _L0_ffn_all

    def _L1_xattn_setup():
        import jax, jax.numpy as jnp
        import numpy as np
        N_HEAD = 16
        key = jax.random.key(seed)
        ks = jax.random.split(key, 5)
        b, l, d = (4, 256, 128)
        dh = d // N_HEAD
        return {'q': jax.random.normal(ks[0], (b, l, d), dtype=jnp.float32), 'kv': jax.random.normal(ks[1], (b, l, d), dtype=jnp.float32), 'Wq': jax.random.normal(ks[2], (d, d), dtype=jnp.float32) * 0.02, 'Wkv': jax.random.normal(ks[3], (2 * dh, d), dtype=jnp.float32) * 0.02, 'Wc': jax.random.normal(ks[4], (d, d), dtype=jnp.float32) * 0.02}
    _L1_xattn_all = _L1_xattn_setup()
    _L1_xattn_in = {k: v for k, v in _L1_xattn_all.items() if k in ('Wq', 'Wkv', 'Wc')}
    del _L1_xattn_all

    def _L1_ffn_setup():
        import jax, jax.numpy as jnp
        import numpy as np
        B, S, D, F, E = (8, 128, 128, 512, 8)
        EPS = 1e-05
        key = jax.random.key(seed)
        ks = jax.random.split(key, 4)
        s = 0.02
        return {'input_features': jax.random.normal(ks[0], (B, S, D), jnp.float32), 'centroids': jax.random.normal(ks[1], (E, D), jnp.float32) * 0.1, 'ln_g': jnp.ones((E, D), jnp.float32), 'ln_b': jnp.zeros((E, D), jnp.float32), 'w1': jax.random.normal(ks[2], (E, D, F), jnp.float32) * s, 'b1': jnp.zeros((E, F), jnp.float32), 'w2': jax.random.normal(ks[3], (E, F, D), jnp.float32) * s, 'b2': jnp.zeros((E, D), jnp.float32)}
    _L1_ffn_all = _L1_ffn_setup()
    _L1_ffn_in = {k: v for k, v in _L1_ffn_all.items() if k in ('centroids', 'ln_g', 'ln_b', 'w1', 'b1', 'w2', 'b2')}
    del _L1_ffn_all
    return {'x': x, 'ctx_1024': ctx_1024, 'L0_xattn_w_sim': _L0_xattn_in['w_sim'], 'L0_xattn_b_sim': _L0_xattn_in['b_sim'], 'L0_xattn_W_qv': _L0_xattn_in['W_qv'], 'L0_xattn_b_qv': _L0_xattn_in['b_qv'], 'L0_ffn_Wqkv': _L0_ffn_in['Wqkv'], 'L0_ffn_q_scale': _L0_ffn_in['q_scale'], 'L0_ffn_k_scale': _L0_ffn_in['k_scale'], 'L0_ffn_Wo': _L0_ffn_in['Wo'], 'L0_ffn_ln_g': _L0_ffn_in['ln_g'], 'L0_ffn_ln_b': _L0_ffn_in['ln_b'], 'L0_ffn_W1': _L0_ffn_in['W1'], 'L0_ffn_b1': _L0_ffn_in['b1'], 'L0_ffn_W2': _L0_ffn_in['W2'], 'L0_ffn_b2': _L0_ffn_in['b2'], 'L1_xattn_Wq': _L1_xattn_in['Wq'], 'L1_xattn_Wkv': _L1_xattn_in['Wkv'], 'L1_xattn_Wc': _L1_xattn_in['Wc'], 'L1_ffn_centroids': _L1_ffn_in['centroids'], 'L1_ffn_ln_g': _L1_ffn_in['ln_g'], 'L1_ffn_ln_b': _L1_ffn_in['ln_b'], 'L1_ffn_w1': _L1_ffn_in['w1'], 'L1_ffn_b1': _L1_ffn_in['b1'], 'L1_ffn_w2': _L1_ffn_in['w2'], 'L1_ffn_b2': _L1_ffn_in['b2']}

def reference(x, ctx_1024, L0_xattn_w_sim, L0_xattn_b_sim, L0_xattn_W_qv, L0_xattn_b_qv, L0_ffn_Wqkv, L0_ffn_q_scale, L0_ffn_k_scale, L0_ffn_Wo, L0_ffn_ln_g, L0_ffn_ln_b, L0_ffn_W1, L0_ffn_b1, L0_ffn_W2, L0_ffn_b2, L1_xattn_Wq, L1_xattn_Wkv, L1_xattn_Wc, L1_ffn_centroids, L1_ffn_ln_g, L1_ffn_ln_b, L1_ffn_w1, L1_ffn_b1, L1_ffn_w2, L1_ffn_b2):
    import jax
    import jax.numpy as jnp

    def _L0_xattn_ref(encoder_hc, decoder_hq, w_sim, b_sim, W_qv, b_qv):
        import jax, jax.numpy as jnp
        import numpy as np
        B, L_ENC, L_DEC, D = (16, 64, 128, 128)
        d = encoder_hc.shape[-1]
        w1, w2, w3 = (w_sim[:d], w_sim[d:2 * d], w_sim[2 * d:])
        Sim = (encoder_hc @ w1)[:, :, None] + (decoder_hq @ w2)[:, None, :] + jnp.einsum('bid,bjd->bij', encoder_hc * w3, decoder_hq) + b_sim[0]
        A = jax.nn.softmax(Sim, axis=2)
        hq_hat = jnp.einsum('bij,bjd->bid', A, decoder_hq)
        Batt = jax.nn.softmax(jnp.max(Sim, axis=2), axis=1)
        hc_bar = jnp.einsum('bi,bid->bd', Batt, encoder_hc)[:, None, :]
        hc_hat = jnp.broadcast_to(hc_bar, encoder_hc.shape)
        feats = jnp.concatenate([encoder_hc, hq_hat, encoder_hc * hq_hat, encoder_hc * hc_hat], axis=-1)
        hcq = feats @ W_qv + b_qv
        return hcq

    def _L0_ffn_ref(x, Wqkv, q_scale, k_scale, Wo, ln_g, ln_b, W1, b1, W2, b2):
        import jax, jax.numpy as jnp
        import numpy as np
        DIM = 128
        DEPTH = 6
        HEADS = 16
        DIM_HEAD = 64
        WINDOW = 32
        INNER = HEADS * DIM_HEAD
        DIM_INNER = int(DIM * 4 * 2 / 3)
        QK_SCALE = 8.0

        def shift_tokens(t):
            a, s = jnp.split(t, 2, -1)
            s = jnp.pad(s, ((0, 0), (1, 0), (0, 0)))[:, :-1]
            return jnp.concatenate([a, s], -1)

        def l2norm(t):
            return t / jnp.maximum(jnp.linalg.norm(t, axis=-1, keepdims=True), 1e-12)

        def rotate_half(x):
            x1, x2 = jnp.split(x, 2, -1)
            return jnp.concatenate([-x2, x1], -1)

        def rotary_tables(n):
            half = jnp.arange(0, DIM_HEAD, 2, dtype=jnp.float32)
            inv_freq = 1.0 / 10000.0 ** (half / DIM_HEAD)
            t = jnp.arange(n, dtype=jnp.float32)
            freqs = t[:, None] * inv_freq[None, :]
            freqs = jnp.concatenate([freqs, freqs], -1)
            base_scale = (half + 0.4 * DIM_HEAD) / (1.4 * DIM_HEAD)
            power = (t - n // 2) / (WINDOW // 2)
            scale = base_scale[None, :] ** power[:, None]
            scale = jnp.concatenate([scale, scale], -1)
            return (freqs, scale)

        def local_attention(q, k, v):
            b, h, n, d = q.shape
            w = WINDOW
            nw = n // w
            bq = q.reshape(b, h, nw, w, d)
            bk = k.reshape(b, h, nw, w, d)
            bv = v.reshape(b, h, nw, w, d)

            def look(t):
                p = jnp.pad(t, ((0, 0), (0, 0), (1, 0), (0, 0), (0, 0)))
                return jnp.concatenate([p[:, :, :nw], p[:, :, 1:]], axis=3)
            bk2, bv2 = (look(bk), look(bv))
            seq = jnp.arange(n).reshape(nw, w)
            seq_p = jnp.pad(seq, ((1, 0), (0, 0)), constant_values=-1)
            jt = jnp.concatenate([seq_p[:nw], seq_p[1:]], axis=1)
            it = seq[:, :, None]
            jb = jt[:, None, :]
            mask = (it < jb) | (it > jb + w) | (jb == -1)
            sim = jnp.einsum('bhwie,bhwje->bhwij', bq, bk2) * QK_SCALE
            sim = jnp.where(mask, -jnp.finfo(sim.dtype).max, sim)
            attn = jax.nn.softmax(sim, -1)
            out = jnp.einsum('bhwij,bhwje->bhwie', attn, bv2)
            return out.reshape(b, h, n, d)

        def attn_layer(x, Wqkv, qs, ksc, Wo):
            b, n, _ = x.shape
            qkv = x @ Wqkv
            q, k, v = jnp.split(qkv, 3, -1)
            sh = lambda t: t.reshape(b, n, HEADS, DIM_HEAD).transpose(0, 2, 1, 3)
            q, k, v = (sh(q), sh(k), sh(v))
            q = l2norm(q) * qs
            k = l2norm(k) * ksc
            freqs, scale = rotary_tables(n)
            cos, sin = (jnp.cos(freqs), jnp.sin(freqs))
            q = q * cos * scale + rotate_half(q) * sin * scale
            inv = 1.0 / scale
            k = k * cos * inv + rotate_half(k) * sin * inv
            out = local_attention(q, k, v)
            out = out.transpose(0, 2, 1, 3).reshape(b, n, INNER)
            return out @ Wo

        def ffn_layer(x, g, bln, W1, b1, W2, b2):
            mu = x.mean(-1, keepdims=True)
            var = ((x - mu) ** 2).mean(-1, keepdims=True)
            xn = (x - mu) / jnp.sqrt(var + 1e-05) * g + bln
            hg = xn @ W1 + b1
            a, gate = jnp.split(hg, 2, -1)
            return a * jax.nn.gelu(gate, approximate=False) @ W2 + b2
        for i in range(DEPTH):
            x = attn_layer(shift_tokens(x), Wqkv[i], q_scale[i], k_scale[i], Wo[i]) + x
            x = ffn_layer(shift_tokens(x), ln_g[i], ln_b[i], W1[i], b1[i], W2[i], b2[i]) + x
        return x

    def _L1_xattn_ref(q, kv, Wq, Wkv, Wc):
        import jax, jax.numpy as jnp
        import numpy as np
        N_HEAD = 16
        b, l, d = q.shape
        h = N_HEAD
        dh = d // h
        qp = jnp.einsum('bld,ed->ble', q, Wq)
        scores = jnp.einsum('bld,bmd->blm', qp, kv)
        idx = jnp.argmax(scores, axis=-1)
        mem = jnp.take_along_axis(kv, idx[..., None], axis=1)
        mkv = jnp.einsum('bld,ed->ble', mem, Wkv)
        mk, mv = jnp.split(mkv, 2, axis=-1)
        qh = qp.reshape(b, l, h, dh).transpose(0, 2, 1, 3)
        scale = 1.0 / np.sqrt(dh).astype(np.float32)
        logits = jnp.einsum('bhld,bmd->bhlm', qh, mk) * scale
        attn = jax.nn.softmax(logits, axis=-1)
        out = jnp.einsum('bhlm,bmd->bhld', attn, mv)
        out = out.transpose(0, 2, 1, 3).reshape(b, l, d)
        return jnp.einsum('bld,ed->ble', out, Wc)

    def _L1_ffn_ref(input_features, centroids, ln_g, ln_b, w1, b1, w2, b2):
        import jax, jax.numpy as jnp
        import numpy as np
        B, S, D, F, E = (8, 128, 128, 512, 8)
        EPS = 1e-05
        x = input_features.reshape(-1, D)
        aff = jax.lax.stop_gradient(x @ centroids.T)
        eid = jnp.argmax(aff, axis=-1)
        alpha = jax.nn.sigmoid(jnp.sum(x * centroids[eid], axis=-1, keepdims=True))
        mu = jnp.mean(x, axis=-1, keepdims=True)
        var = jnp.mean((x - mu) ** 2, axis=-1, keepdims=True)
        xn = (x - mu) * jax.lax.rsqrt(var + EPS)
        xln = xn * ln_g[eid] + ln_b[eid]
        onehot = jax.nn.one_hot(eid, E, dtype=x.dtype)
        ffn = jnp.zeros_like(x)
        for e in range(E):
            h = jax.nn.relu(xln @ w1[e] + b1[e])
            ffn = ffn + onehot[:, e:e + 1] * (h @ w2[e] + b2[e])
        out = x + alpha * ffn
        return out.reshape(input_features.shape)
    x = x + _L0_xattn_ref(_layernorm(x, axis=-1), ctx_1024, L0_xattn_w_sim, L0_xattn_b_sim, L0_xattn_W_qv, L0_xattn_b_qv)
    x = x + _L0_ffn_ref(_layernorm(x, axis=-1), L0_ffn_Wqkv, L0_ffn_q_scale, L0_ffn_k_scale, L0_ffn_Wo, L0_ffn_ln_g, L0_ffn_ln_b, L0_ffn_W1, L0_ffn_b1, L0_ffn_W2, L0_ffn_b2)
    x = x + _L1_xattn_ref(_layernorm(x, axis=-1), ctx_1024, L1_xattn_Wq, L1_xattn_Wkv, L1_xattn_Wc)
    x = x + _L1_ffn_ref(_layernorm(x, axis=-1), L1_ffn_centroids, L1_ffn_ln_g, L1_ffn_ln_b, L1_ffn_w1, L1_ffn_b1, L1_ffn_w2, L1_ffn_b2)
    return x

_drawn_inputs = setup_inputs


def setup_inputs(seed=0):
    import zlib

    import numpy as np

    out = dict(_drawn_inputs(seed))
    spreads = {'L0_ffn_q_scale': (1.0, 0.6),
     'L0_ffn_k_scale': (1.0, 0.6),
     'L0_ffn_ln_g': (1.0, 0.6),
     'L0_ffn_ln_b': (0.0, 0.8),
     'L0_ffn_b1': (0.0, 0.8),
     'L0_ffn_b2': (0.0, 0.1),
     'L1_ffn_ln_g': (1.0, 0.6),
     'L1_ffn_ln_b': (0.0, 2.0),
     'L1_ffn_b1': (0.0, 2.0),
     'L1_ffn_b2': (0.0, 0.286)}
    factors = {'L0_ffn_W1': 3.615,
     'L0_ffn_W2': 3.51,
     'L1_xattn_Wq': 8.0,
     'L1_xattn_Wkv': 4.044,
     'L1_xattn_Wc': 3.195,
     'L1_ffn_w1': 3.251}
    for name, (base, spread) in spreads.items():
        noise = np.random.default_rng([zlib.crc32(name.encode()), seed]).standard_normal(out[name].shape)
        drawn = base * np.exp(spread * noise) if base else spread * noise
        out[name] = jnp.asarray(drawn.astype(out[name].dtype))
    for name, factor in factors.items():
        out[name] = (out[name] * factor).astype(out[name].dtype)
    return out
```

```python
from contextlib import ExitStack

import numpy as np

import concourse.bass as bass
from concourse import mybir

fp32 = mybir.dt.float32
bf16 = mybir.dt.bfloat16
u32 = mybir.dt.uint32
ALU = mybir.AluOpType
ACT = mybir.ActivationFunctionType
AX = mybir.AxisListType

P = 128
B = 4
TILES = 4
NT = B * TILES
SEQ = TILES * P
CTX = 77
EPS = 1e-5

LAYERS = 6
HEADS = 16
DH = 64
PAIRS = HEADS // 2
WIN = 32
INNER = HEADS * DH
KEYS = WIN + P
HID = 341
HCH = 3
HREST = HID - 2 * P
MASKED = -1e30

XHEADS = 16
XDH = 8
EXPERTS = 8
FF = 512
FCH = FF // P

C_IDENT = 0
C_ONES = C_IDENT + P
C_ROW0 = C_ONES + P
C_BAND = C_ROW0 + P
C_IOTA = C_BAND + 2 * KEYS
C_HEADS = C_IOTA + 80
C_ROPE = C_HEADS + XHEADS
C_ALL = C_ROPE + TILES * 4 * DH


def constants():
    c = np.zeros((P, C_ALL), np.float32)
    c[:, C_IDENT:C_IDENT + P] = np.eye(P)
    c[:, C_ONES:C_ONES + P] = 1.0
    c[0, C_ROW0:C_ROW0 + P] = 1.0
    back = (np.arange(P)[:, None] + WIN) - np.arange(KEYS)[None, :]
    band = np.where((back < 0) | (back > WIN), MASKED, 0.0)
    c[:, C_BAND:C_BAND + KEYS] = band
    c[:, C_BAND + KEYS:C_BAND + 2 * KEYS] = band
    c[:, C_IOTA:C_IOTA + 80] = np.arange(80)[None, :]
    c[:, C_HEADS:C_HEADS + XHEADS] = np.arange(P)[:, None] // XDH == np.arange(XHEADS)[None, :]
    half = np.arange(0, DH, 2, dtype=np.float32)
    inv = (np.float32(1.0) / np.float32(10000.0) ** (half / np.float32(DH))).astype(np.float32)
    t = np.arange(SEQ, dtype=np.float32)
    freqs = (t[:, None] * inv[None, :]).astype(np.float32).astype(np.float64)
    base = (half + 0.4 * DH) / (1.4 * DH)
    scale = base[None, :].astype(np.float64) ** ((t - SEQ // 2) / (WIN // 2))[:, None].astype(np.float64)
    cos, sin = np.cos(freqs), np.sin(freqs)
    tab = np.stack([
        np.concatenate([cos * scale, cos * scale], 1) * 8.0,
        np.concatenate([sin * scale, -sin * scale], 1) * 8.0,
        np.concatenate([cos / scale, cos / scale], 1),
        np.concatenate([sin / scale, -sin / scale], 1),
    ], 1)
    c[:, C_ROPE:] = tab.reshape(TILES, P, 4 * DH).transpose(1, 0, 2).reshape(P, -1)
    return c


class Memory:

    def __init__(self, nc, ctx, part):
        self.nc, self.ctx, self.part, self.sems = nc, ctx, part, []

    def sb(self, name, shape, dt=fp32):
        return self.ctx.enter_context(self.nc.sbuf_tensor(f"{self.part}_{name}", shape, dt))

    def bank(self, name):
        return self.ctx.enter_context(self.nc.psum_tensor(f"{self.part}_bank_{name}", [P, 512], fp32))

    def sem(self, name):
        s = self.ctx.enter_context(self.nc.semaphore(f"{self.part}_{name}"))
        self.sems.append(s)
        return s

    def clear_sems(self):
        numbers = [s.num for s in self.sems]
        with self.nc.Block() as block:
            @block.gpsimd
            def _(pool):
                pool.sem_clear(range(min(numbers), max(numbers) + 1))


def wait(eng, sem, value):
    if isinstance(value, int) and value <= 0:
        return
    eng.wait_ge(sem, value)


def apart(eng):
    eng.nop(nofuse=True)


def cols(a, start, n):
    return a[:, bass.ds(start, n)]


def split(a, inner):
    return a.rearrange("p (a b) -> p a b", b=inner)


def repeat_mid(a, n):
    return a.rearrange("p (o c) -> p o c", o=1).to_broadcast([a.shape[0], n, a.shape[1]])


def repeat_last(a, n):
    return a.rearrange("p (h o) -> p h o", o=1).to_broadcast([a.shape[0], a.shape[1], n])


def cross_attention(nc, const, X, XS, ctx_h, w_sim, b_sim, W_qv, b_qv, x_h, const_h):
    with ExitStack() as es:
        m = Memory(nc, es, "a")
        xv, sv = X[:, :], XS[:, :]
        w3 = m.sb("w_sim", [P, 3])
        bsim = m.sb("b_sim", [1, 1])
        wqv = m.sb("w_qv", [P, 4 * P])
        bqv = m.sb("b_qv", [1, P])
        cb = m.sb("ctx", [CTX, P])
        cT = m.sb("ctx_t", [P, CTX])
        gT = m.sb("keys_t", [P, CTX])
        urow = m.sb("key_bias", [1, CTX])
        st = m.sb("stats", [P, TILES, 6])
        mv = m.sb("mean_var", [P, TILES, 2])
        ve = m.sb("var_eps", [P, TILES])
        rs = m.sb("rstd", [P, TILES])
        st2 = m.sb("stats2", [P, TILES, 6])
        mv2 = m.sb("mean_var2", [P, TILES, 2])
        ve2 = m.sb("var_eps2", [P, TILES])
        rs2 = m.sb("rstd2", [P, TILES])
        mhalf = m.sb("minus_half", [P, TILES])
        e = m.sb("normed", [P, TILES, P])
        eT = m.sb("normed_t", [P, SEQ])
        nm = m.sb("neg_max", [P, TILES])
        mx = m.sb("max_own", [P, 1])
        mxa = m.sb("max_all", [P, 1])
        nmx = m.sb("neg_max_all", [P, 1])
        pr = m.sb("probs", [P, TILES, CTX])
        sm = m.sb("sums", [P, TILES])
        ri = m.sb("inv_sums", [P, TILES])
        prn = m.sb("probs_normed", [P, TILES, CTX])
        pT = m.sb("probs_t", [CTX, SEQ])
        hT = m.sb("hat_t", [P, SEQ])
        ehT = m.sb("normed_hat_t", [P, SEQ])
        bw = m.sb("batt", [P, TILES])
        rb = m.sb("inv_batt_sum", [P, 1])
        hc = m.sb("hc_bar", [P, 1])
        weff = m.sb("w_eff", [P, P])
        bk_eT, bk_c, bk_u, bk_s, bk_p, bk_h, bk_b, bk_y = [
            m.bank(n) for n in ("nt", "ct", "u", "s", "pt", "h", "b", "y")]

        x_in, const_in, w_in, ctx_in = [m.sem(n) for n in ("x_in", "const_in", "w_in", "ctx_in")]
        half_set = m.sem("half_set")
        dve_own = m.sem("vector_step")
        pool_own = m.sem("pool_step")
        stats, rstd, normed, eT_full, eT_done = [m.sem(n) for n in ("stats_", "rstd_", "normed_", "nt_full", "nt_done")]
        cT_full, cT_done, gT_done, u_full, u_done = [m.sem(n) for n in ("ct_full", "ct_done", "gt_done", "u_full", "u_done")]
        s_full, s_max, s_exp, p_normed, pT_full, pT_done = [
            m.sem(n) for n in ("s_full", "s_max", "s_exp", "p_normed", "pt_full", "pt_done")]
        h_full, hT_done, ehT_done = [m.sem(n) for n in ("h_full", "ht_done", "eht_done")]
        max_own, max_all, max_neg, batt, b_full, weff_done = [
            m.sem(n) for n in ("max_own_", "max_all_", "max_neg_", "batt_", "b_full", "weff_done")]
        y_full, x_done, xs_stats, stats2, rstd2, xs_done = [
            m.sem(n) for n in ("y_full", "x_done", "xs_stats", "stats2_", "rstd2_", "xs_done")]

        ident = const[:, C_IDENT:C_IDENT + P]
        ones = const[:, C_ONES:C_ONES + P]
        NW = 6

        with nc.Block() as block:
            @block.sync
            def _(sp):
                sp.dma_start(split(xv, P), x_h.rearrange("b (t p) d -> p (b t) d", p=P)).then_inc(x_in, 16)
                sp.dma_start(const[:, :], const_h).then_inc(const_in, 16)
                for k in range(3):
                    sp.dma_start(w3[:, k:k + 1], w_sim[k * P:(k + 1) * P].rearrange("(p o) -> p o", o=1)).then_inc(w_in, 16)
                sp.dma_start(bsim[:, :], b_sim.rearrange("(p o) -> p o", o=1)).then_inc(w_in, 16)
                sp.dma_start(split(wqv[:, :], P), W_qv.rearrange("(k p) n -> p k n", p=P)).then_inc(w_in, 16)
                sp.dma_start(bqv[:, :], b_qv.rearrange("(o p) -> o p", o=1)).then_inc(w_in, 16)
                with sp.Fori(0, B) as b:
                    sp.wait_ge(h_full, b)
                    sp.dma_start(cb[:, :], ctx_h[bass.ds(b, 1), :, :].rearrange("o j d -> (o j) d")).then_inc(ctx_in, 16)

            @block.gpsimd
            def _(pool):
                nc.gpsimd.memset(mhalf[:, :], -0.5).then_inc(half_set, 1)
                pool.wait_ge(half_set, 1)
                with pool.Fori(0, B) as b:
                    pool.wait_ge(stats, b + 1)
                    apart(pool)
                    nc.gpsimd.tensor_scalar(ve[:, :], mv[:, :, 1], EPS, None, ALU.add).then_inc(pool_own, 1)
                    pool.wait_ge(pool_own, b * 2 + 1)
                    pool.wait_ge(normed, b)
                    nc.gpsimd.tensor_tensor(out=rs[:, :], in0=ve[:, :], in1=mhalf[:, :], op=ALU.pow).then_inc(rstd, 1)
                    pool.wait_ge(max_own, b + 1)
                    pool.wait_ge(max_neg, b)
                    apart(pool)
                    nc.gpsimd.partition_all_reduce(mxa[:, :], mx[:, :], P, bass.bass_isa.ReduceOp.max).then_inc(max_all, 1)
                    pool.wait_ge(stats2, b + 1)
                    apart(pool)
                    nc.gpsimd.tensor_scalar(ve2[:, :], mv2[:, :, 1], EPS, None, ALU.add).then_inc(pool_own, 1)
                    pool.wait_ge(pool_own, b * 2 + 2)
                    pool.wait_ge(xs_done, b)
                    nc.gpsimd.tensor_tensor(out=rs2[:, :], in0=ve2[:, :], in1=mhalf[:, :], op=ALU.pow).then_inc(rstd2, 1)

            @block.scalar
            def _(act):
                act.wait_ge(const_in, 16)
                with act.Fori(0, B) as b:
                    act.wait_ge(cT_full, b + 1)
                    act.wait_ge(u_full, b)
                    act.wait_ge(gT_done, b + 1)
                    nc.scalar.activation(cT[:, :], bk_c[:, 0:CTX], ACT.Copy).then_inc(cT_done, 1)
                    act.wait_ge(eT_full, b + 1)
                    act.wait_ge(y_full, b)
                    act.wait_ge(ehT_done, b)
                    nc.scalar.activation(eT[:, :], bk_eT[:, :], ACT.Copy).then_inc(eT_done, 1)
                    act.wait_ge(s_max, b + 1)
                    act.wait_ge(p_normed, b)
                    for t in range(TILES):
                        last = nc.scalar.activation(pr[:, t, :], bk_s[:, t * CTX:(t + 1) * CTX], ACT.Exp,
                                                    bias=nm[:, t:t + 1], accum_out=sm[:, t:t + 1])
                    last.then_inc(s_exp, 1)
                    act.wait_ge(max_neg, b + 1)
                    act.wait_ge(b_full, b)
                    nc.scalar.activation(bw[:, :], nm[:, :], ACT.Exp, bias=nmx[:, :], scale=-1.0).then_inc(batt, 1)
                    act.wait_ge(pT_full, b + 1)
                    act.wait_ge(h_full, b)
                    nc.scalar.activation(pT[:, :], bk_p[0:CTX, :], ACT.Copy).then_inc(pT_done, 1)
                    act.wait_ge(h_full, b + 1)
                    act.wait_ge(y_full, b)
                    nc.scalar.activation(hT[:, :], bk_h[:, :], ACT.Copy).then_inc(hT_done, 1)

            @block.vector
            def _(dve):
                dve.wait_ge(x_in, 16)
                dve.wait_ge(const_in, 16)
                dve.wait_ge(w_in, 16 * NW)
                with dve.Fori(0, B) as b:
                    own = 4

                    def step(k):
                        dve.wait_ge(dve_own, b * own + k)
                    xb = cols(xv, b * SEQ, SEQ)
                    apart(dve)
                    for t in range(TILES):
                        last = nc.vector.bn_stats(st[:, t, :], cols(xv, b * SEQ + t * P, P))
                    last.then_inc(dve_own, 1)
                    step(1)
                    dve.wait_ge(rstd, b)
                    apart(dve)
                    for t in range(TILES):
                        last = nc.vector.bn_aggr(mv[:, t, :], st[:, t, :])
                    last.then_inc(stats, 1)
                    dve.wait_ge(cT_full, b + 1)
                    dve.wait_ge(s_full, b)
                    nc.vector.tensor_scalar(gT[:, :], bk_c[:, 0:CTX], w3[:, 2:3], w3[:, 0:1], ALU.mult, ALU.add).then_inc(gT_done, 1)
                    dve.wait_ge(rstd, b + 1)
                    dve.wait_ge(stats, b + 1)
                    dve.wait_ge(b_full, b)
                    for t in range(TILES):
                        last = nc.vector.tensor_scalar(e[:, t, :], cols(xv, b * SEQ + t * P, P), mv[:, t, 0:1],
                                                       rs[:, t:t + 1], ALU.subtract, ALU.mult)
                    last.then_inc(normed, 1)
                    dve.wait_ge(u_full, b + 1)
                    dve.wait_ge(s_full, b)
                    nc.vector.tensor_scalar(urow[:, :], bk_u[0:1, 0:CTX], bsim[:, :], None, ALU.add).then_inc(u_done, 1)
                    dve.wait_ge(s_full, b + 1)
                    dve.wait_ge(batt, b)
                    dve.wait_ge(max_all, b)
                    scores = bk_s[:, 0:TILES * CTX]
                    nc.vector.tensor_reduce(mx[:, :], scores, AX.X, ALU.max).then_inc(max_own, 1)
                    nc.vector.tensor_reduce(nm[:, :], split(scores, CTX), AX.X, ALU.max, negate=True).then_inc(s_max, 1)
                    dve.wait_ge(s_exp, b + 1)
                    nc.vector.reciprocal(ri[:, :], sm[:, :]).then_inc(dve_own, 1)
                    step(2)
                    dve.wait_ge(pT_full, b)
                    nc.vector.tensor_tensor(prn[:, :, :], pr[:, :, :], repeat_last(ri[:, :], CTX), ALU.mult).then_inc(p_normed, 1)
                    dve.wait_ge(max_all, b + 1)
                    nc.vector.tensor_scalar(nmx[:, :], mxa[:, :], -1.0, None, ALU.mult).then_inc(max_neg, 1)
                    dve.wait_ge(b_full, b + 1)
                    nc.vector.reciprocal(rb[:, :], bk_b[:, 1:2]).then_inc(dve_own, 1)
                    step(3)
                    nc.vector.tensor_scalar(hc[:, :], bk_b[:, 0:1], rb[:, :], None, ALU.mult).then_inc(dve_own, 1)
                    step(4)
                    dve.wait_ge(y_full, b)
                    nc.vector.scalar_tensor_tensor(weff[:, :], wqv[:, 3 * P:4 * P], hc[:, :], wqv[:, 0:P],
                                                   ALU.mult, ALU.add).then_inc(weff_done, 1)
                    dve.wait_ge(h_full, b + 1)
                    dve.wait_ge(hT_done, b + 1)
                    nc.vector.tensor_tensor(ehT[:, :], bk_h[:, :], eT[:, :], ALU.mult).then_inc(ehT_done, 1)
                    dve.wait_ge(y_full, b + 1)
                    nc.vector.tensor_tensor(xb, bk_y[:, :], xb, ALU.add).then_inc(x_done, 1)
                    dve.wait_ge(x_done, b + 1)
                    apart(dve)
                    for t in range(TILES):
                        last = nc.vector.bn_stats(st2[:, t, :], cols(xv, b * SEQ + t * P, P))
                    last.then_inc(xs_stats, 1)
                    dve.wait_ge(xs_stats, b + 1)
                    apart(dve)
                    for t in range(TILES):
                        last = nc.vector.bn_aggr(mv2[:, t, :], st2[:, t, :])
                    last.then_inc(stats2, 1)
                    dve.wait_ge(rstd2, b + 1)
                    dve.wait_ge(stats2, b + 1)
                    for t in range(TILES):
                        last = nc.vector.tensor_scalar(cols(sv, b * SEQ + t * P, P), cols(xv, b * SEQ + t * P, P),
                                                       mv2[:, t, 0:1], rs2[:, t:t + 1], ALU.subtract, ALU.mult)
                    last.then_inc(xs_done, 1)

            @block.tensor
            def _(pe):
                pe.wait_ge(const_in, 16)
                pe.wait_ge(w_in, 16 * NW)
                with pe.Fori(0, B) as b:
                    pe.wait_ge(ctx_in, 16 * b + 16)
                    pe.wait_ge(gT_done, b)
                    pe.wait_ge(cT_done, b)
                    nc.tensor.transpose(bk_c[:, 0:CTX], cb[:, :], ident[0:CTX, 0:CTX]).then_inc(cT_full, 1)
                    pe.wait_ge(cT_done, b + 1)
                    pe.wait_ge(u_done, b)
                    nc.tensor.matmul(bk_u[0:1, 0:CTX], w3[:, 1:2], cT[:, :], start=True, stop=True).then_inc(u_full, 1)
                    pe.wait_ge(normed, b + 1)
                    pe.wait_ge(eT_done, b)
                    for t in range(TILES):
                        last = nc.tensor.transpose(bk_eT[:, t * P:(t + 1) * P], e[:, t, :], ident)
                    last.then_inc(eT_full, 1)
                    pe.wait_ge(eT_done, b + 1)
                    pe.wait_ge(gT_done, b + 1)
                    pe.wait_ge(u_done, b + 1)
                    pe.wait_ge(s_exp, b)
                    for t in range(TILES):
                        out = bk_s[:, t * CTX:(t + 1) * CTX]
                        nc.tensor.matmul(out, eT[:, t * P:(t + 1) * P], gT[:, :], start=True, stop=False)
                        last = nc.tensor.matmul(out, ones[0:1, :], urow[:, :], start=False, stop=True)
                    last.then_inc(s_full, 1)
                    pe.wait_ge(p_normed, b + 1)
                    pe.wait_ge(pT_done, b)
                    for t in range(TILES):
                        last = nc.tensor.transpose(bk_p[0:CTX, t * P:(t + 1) * P], prn[:, t, :], ident)
                    last.then_inc(pT_full, 1)
                    pe.wait_ge(batt, b + 1)
                    pe.wait_ge(weff_done, b)
                    for t in range(TILES):
                        nc.tensor.matmul(bk_b[:, 0:1], e[:, t, :], bw[:, t:t + 1], start=(t == 0), stop=(t == TILES - 1))
                    for t in range(TILES):
                        last = nc.tensor.matmul(bk_b[:, 1:2], ones, bw[:, t:t + 1], start=(t == 0), stop=(t == TILES - 1))
                    last.then_inc(b_full, 1)
                    pe.wait_ge(pT_done, b + 1)
                    pe.wait_ge(hT_done, b)
                    pe.wait_ge(ehT_done, b)
                    nc.tensor.matmul(bk_h[:, :], cb[:, :], pT[:, :], start=True, stop=True).then_inc(h_full, 1)
                    pe.wait_ge(weff_done, b + 1)
                    pe.wait_ge(hT_done, b + 1)
                    pe.wait_ge(ehT_done, b + 1)
                    pe.wait_ge(x_done, b)
                    for t in range(TILES):
                        tok = slice(t * P, (t + 1) * P)
                        nc.tensor.matmul(bk_y[:, tok], eT[:, tok], weff[:, :], start=True, stop=False)
                        nc.tensor.matmul(bk_y[:, tok], hT[:, tok], wqv[:, P:2 * P], start=False, stop=False)
                        nc.tensor.matmul(bk_y[:, tok], ehT[:, tok], wqv[:, 2 * P:3 * P], start=False, stop=False)
                        last = nc.tensor.matmul(bk_y[:, tok], ones[0:1, :], bqv[:, :], start=False, stop=True)
                    last.then_inc(y_full, 1)
        m.clear_sems()



def turn_steps():
    def tile(t):
        return t // TILES, t % TILES

    steps = []
    for t in range(TILES):
        ahead2, ahead, behind, behind2 = [tile(t + n) for n in (2, 1, -1, -2)]
        extra = {
            0: [("out_t", *behind, 0), ("rope", *ahead, 0), ("project", *ahead, 2)],
            1: [("project", *ahead, 3)],
            2: [("out_t", *behind, 1), ("rope", *ahead, 1), ("up", *behind2, 0)],
            3: [("out", *behind, 0), ("heads_t", *ahead, 0), ("up", *behind2, 1)],
            4: [("shift", *behind, 0), ("heads_t", *ahead, 1), ("project", *ahead, 4)],
            5: [("back", *behind, 0), ("project", *ahead, 5), ("table", *ahead2, 0)],
            6: [("norm", *behind, 0), ("heads_t", *ahead, 2), ("project", *ahead2, 0)],
            7: [("norm_t", *behind, 0), ("heads_t", *ahead, 3), ("project", *ahead2, 1)],
        }
        first = {p: [] for p in range(PAIRS)}
        if t == 1:
            extra[4].append(("gelu", -1, 0, 0))
            extra[4].append(("stage", 1, 0, 0))
            extra[5].append(("hidden", -1, 0, 0))
            extra[6].append(("hidden", -1, 1, 0))
            first[7] = [("gate", -1, 0, 0)]
        if t == 2:
            first[0] = [("down", -1, 0, 0)]
            first[1] = [("gate", -1, 1, 0)]
            first[2] = [("down", -1, 1, 0)]
            first[5] = [("stage_t", 1, 0, 0)]
            extra[3].append(("hidden", -1, 2, 0))
            extra[4].append(("hidden", -1, 3, 0))
            first[6] = [("gate", -1, 2, 0)]
            first[7] = [("down", -1, 2, 0)]
        if t == 3:
            first[1] = [("gate", -1, 3, 0)]
            first[2] = [("down", -1, 3, 0)]
        for p in range(PAIRS):
            steps.append(("scores", 0, t, p))
            steps += first[p]
            steps.append(("probs_t", 0, t, p - 1) if p >= 1 else ("probs_t", *behind, PAIRS - 1))
            steps.append(("pv", 0, t, p - 2) if p >= 2 else ("pv", *behind, PAIRS - 2 + p))
            steps += extra[p]
    return steps


TURN = turn_steps()
LEAD_IN = [("stage", 1, 0, 0), ("stage_t", 1, 0, 0)] + [s for s in TURN if s[1] == 1 and s[0] not in ("stage", "stage_t")]
FIRST = [s for s in TURN if s[1] >= 0]
LEAD_OUT = [s for s in TURN if s[1] < 0]
TURNS = LAYERS * B

BANK_STEPS = {
    "proj0": lambda s: s[0] in ("project", "up") and s[3] % 2 == 0,
    "proj1": lambda s: s[0] in ("project", "up") and s[3] % 2 == 1,
    "turned": lambda s: s[0] in ("stage_t", "heads_t", "out_t", "gate"),
    "sum": lambda s: s[0] in ("out", "shift", "back", "norm_t", "down"),
}


def bank_before(part, k, bank):
    uses = BANK_STEPS[bank]
    for j in range(k - 1, -1, -1):
        if uses(part[j]):
            return part[j], 0
    earlier = {id(LEAD_IN): [], id(FIRST): LEAD_IN, id(TURN): TURN, id(LEAD_OUT): TURN}[id(part)]
    for s in reversed(earlier):
        if uses(s):
            return s, 1
    return None


W_QKV = 0
W_O = 3 * INNER
W_UP = W_O + PAIRS * P
W_DOWN = W_UP + 2 * HID
W_ALL = W_DOWN + HCH * P


def windowed_layers(nc, const, XS, Wqkv, q_scale, k_scale, Wo, ln_g, ln_b, W1, b1, W2, b2):
    with ExitStack() as es:
        m = Memory(nc, es, "b")
        xs = XS[:, :]
        wts = m.sb("weights", [P, 2 * W_ALL])
        b1b = m.sb("b1", [P, 2 * 2 * HID])
        b2b = m.sb("b2", [P, 2 * P])
        qk_scale = m.sb("qk_scale", [P, LAYERS * 2 * DH])
        lng = m.sb("ln_g", [P, LAYERS])
        lnb = m.sb("ln_b", [P, LAYERS])
        band = m.sb("band", [P, 2 * KEYS], bf16)
        identb = m.sb("ident", [P, P], bf16)
        mhalf = m.sb("minus_half", [P, HEADS])
        rope = m.sb("rope", [P, 2, 4, DH])
        xin = m.sb("staged", [P, SEQ])
        xT = m.sb("staged_t", [P, SEQ + 1])
        plain = m.sb("plain", [P, 2, INNER])
        moved = m.sb("moved", [P, 2, INNER])
        squares = m.sb("squares", [P, 2, INNER])
        ss = m.sb("norm2", [P, 2, HEADS])
        ssc = m.sb("norm2_clamped", [P, 2, HEADS])
        rn = m.sb("inv_norm", [P, 2, HEADS])
        turned = m.sb("rotated", [P, 2, INNER])
        qT = m.sb("q_t", [P, 2, PAIRS, 2, P])
        kT = m.sb("k_t", [P, PAIRS, WIN + SEQ])
        V = m.sb("v", [P, TILES, HEADS, DH + 1])
        nmax = m.sb("neg_max", [P, 2, 2])
        LEFT = 3 * WIN
        probs = m.sb("probs", [P, 2, 2, LEFT + KEYS])
        pT = m.sb("probs_t", [P, 2, 2 * P + 2 * WIN])
        rsum = m.sb("inv_sum", [P, 2, 4])
        O = m.sb("attended", [P, INNER])
        OT = m.sb("attended_t", [P, PAIRS * P])
        x1 = m.sb("x1", [P, SEQ])
        x1b = m.sb("x1_b2", [P, 2 * SEQ])
        x1T = m.sb("x1_t", [P, SEQ + 1])
        xb = m.sb("shifted", [P, P])
        st = m.sb("stats", [P, 6])
        mv = m.sb("mean_var", [P, 2])
        ve = m.sb("var_eps", [P, 1])
        rstd = m.sb("rstd", [P, 1])
        xn = m.sb("normed", [P, P])
        xnT = m.sb("normed_t", [P, P])
        gate = m.sb("gate", [P, TILES, HID])
        lin = m.sb("linear", [P, TILES, HID])
        hid = m.sb("hidden", [P, 2, HID])
        hidT = m.sb("hidden_t", [P, HCH * P])

        bk_proj = [m.bank("proj0"), m.bank("proj1")]
        bk_turn = m.bank("turned")
        bk_s = [m.bank("scores0"), m.bank("scores1")]
        bk_pT = m.bank("probs_t")
        bk_o = m.bank("attended")
        bk_sum = m.bank("sum")

        names = ("const_in", "w_in", "b_set", "pool_set", "pool_own", "staged", "stage_t_full", "stage_t_done",
                 "table_done", "proj_full", "sq_done", "v_done", "rope_mul", "ss_done", "rope_done",
                 "heads_t_full", "heads_t_done", "s_full", "s_max", "s_exp", "pt_full", "pt_done", "pv_done",
                 "o_done", "out_t_full", "out_t_done", "out_full", "x1_done", "x1b_done", "shift_full",
                 "shift_done", "back_full", "back_done", "mv_done", "rstd_done", "xn_done", "norm_t_full",
                 "norm_t_done", "up_full", "up_done", "gelu_done", "hid_done", "gate_full", "gate_done",
                 "down_full", "xs_done")
        s = {n: m.sem(n) for n in names}
        (const_in, w_in, b_set, pool_set, pool_own, staged, stage_t_full, stage_t_done, table_done, proj_full,
         sq_done, v_done, rope_mul, ss_done, rope_done, heads_t_full, heads_t_done, s_full, s_max, s_exp,
         pt_full, pt_done, pv_done, o_done, out_t_full, out_t_done, out_full, x1_done, x1b_done, shift_full,
         shift_done, back_full, back_done, mv_done, rstd_done, xn_done, norm_t_full, norm_t_done, up_full,
         up_done, gelu_done, hid_done, gate_full, gate_done, down_full, xs_done) = (s[n] for n in names)

        ident = const[:, C_IDENT:C_IDENT + P]
        NW = 7
        NC = 4
        HID_AHEAD = TILES
        DONE_AHEAD = 12

        def emptied(step, turn):
            kind, d, t, k = step
            j = turn + d
            u = 4 * j + t
            return {
                "project": lambda: [(rope_mul, 4 * u + k + 1)] if k < 4 else [(v_done, 2 * u + k - 3)],
                "up": lambda: [(up_done, 2 * u + k + 1)],
                "stage_t": lambda: [(stage_t_done, j + 1)],
                "heads_t": lambda: [(heads_t_done, 4 * u + k + 1)],
                "out_t": lambda: [(out_t_done, 2 * u + k + 1)],
                "shift": lambda: [(shift_done, u + 1)],
                "back": lambda: [(back_done, u + 1)],
                "norm_t": lambda: [(norm_t_done, u + 1)],
                "gate": lambda: [(gate_done, u + 1)],
                "out": lambda: [(x1_done, u + 1)],
                "down": lambda: [(xs_done, DONE_AHEAD + u + 1)],
            }[kind]()

        def parts(eng):
            yield LEAD_IN, -1
            yield FIRST, 0
            with eng.Fori(1, TURNS) as i:
                yield TURN, i
            yield LEAD_OUT, TURNS

        def layer_of(j):
            return j // B

        def slot_of(j):
            return (j // B) % 2

        def tile_at(j, t):
            return (j % B) * SEQ + t * P

        with nc.Block() as block:
            @block.sync
            def _(sp):
                sp.dma_start(split(qk_scale[:, :], DH).rearrange("p (l k) d -> p l k d", k=2)[:, :, 0, :],
                             q_scale.rearrange("(o l) d -> o l d", o=1).to_broadcast([P, LAYERS, DH])).then_inc(const_in, 16)
                sp.dma_start(split(qk_scale[:, :], DH).rearrange("p (l k) d -> p l k d", k=2)[:, :, 1, :],
                             k_scale.rearrange("(o l) d -> o l d", o=1).to_broadcast([P, LAYERS, DH])).then_inc(const_in, 16)
                with nc.allow_non_contiguous_dma(reason="one column per layer"):
                    sp.dma_start(lng[:, :], ln_g.rearrange("l p -> p l")).then_inc(const_in, 16)
                    sp.dma_start(lnb[:, :], ln_b.rearrange("l p -> p l")).then_inc(const_in, 16)
                def load(l, to):
                    def src(a):
                        return a[bass.ds(l, 1)]
                    def dst(buf, width, start, n):
                        return cols(buf, to * width + start, n)
                    sp.dma_start(dst(wts, W_ALL, W_QKV, 3 * INNER), src(Wqkv).rearrange("o p n -> (o p) n")).then_inc(w_in, 16)
                    sp.dma_start(split(dst(wts, W_ALL, W_O, PAIRS * P), P),
                                 src(Wo).rearrange("o (k p) n -> (o p) k n", p=P)).then_inc(w_in, 16)
                    sp.dma_start(dst(wts, W_ALL, W_UP, 2 * HID), src(W1).rearrange("o p n -> (o p) n")).then_inc(w_in, 16)
                    sp.dma_start(split(dst(wts, W_ALL, W_DOWN, 2 * P), P),
                                 W2[bass.ds(l, 1), 0:2 * P, :].rearrange("o (k p) n -> (o p) k n", p=P)).then_inc(w_in, 16)
                    sp.dma_start(wts[0:HREST, bass.ds(to * W_ALL + W_DOWN + 2 * P, P)],
                                 W2[bass.ds(l, 1), 2 * P:HID, :].rearrange("o p n -> (o p) n")).then_inc(w_in, 16)
                    sp.dma_start(dst(b1b, 2 * HID, 0, 2 * HID), src(b1).to_broadcast([P, 2 * HID])).then_inc(w_in, 16)
                    sp.dma_start(dst(b2b, P, 0, P), src(b2).to_broadcast([P, P])).then_inc(w_in, 16)

                load(0, 0)
                with sp.Fori(0, LAYERS) as l:
                    sp.wait_ge(w_in, (l + 1) * NW * 16)
                    sp.wait_ge(xs_done, l * NT + DONE_AHEAD)
                    load((l + 1) % LAYERS, (l + 1) % 2)
                sp.wait_ge(w_in, (LAYERS + 1) * NW * 16)

            @block.gpsimd
            def _(pool):
                for n, (a, v) in enumerate(((mhalf[:, :], -0.5), (xT[P // 2:P, 0:1], 0.0), (x1T[P // 2:P, 0:1], 0.0),
                             (qT[:, :, :, :, :], 0.0), (kT[:, :, 0:WIN], 0.0), (probs[:, :, :, 0:LEFT], 0.0),
                             (V[:, :, :, DH:DH + 1], 1.0))):
                    wait(pool, pool_set, n)
                    nc.gpsimd.memset(a, v).then_inc(pool_set, 1)
                pool.wait_ge(pool_set, 7)
                pool.wait_ge(const_in, 16 * NC)
                made = [0]

                def table(i, d, t, k):
                    j = i + d
                    u = 4 * j + t
                    wait(pool, rope_mul, 4 * (u - 1))
                    base = split(const[:, C_ROPE + t * 4 * DH:C_ROPE + (t + 1) * 4 * DH], DH)
                    apart(pool)
                    for qk in range(2):
                        sc = cols(qk_scale, (layer_of(j) % LAYERS) * 2 * DH + qk * DH, DH)
                        last = nc.gpsimd.tensor_tensor(out=rope[:, t % 2, 2 * qk:2 * qk + 2, :],
                                                       in0=base[:, 2 * qk:2 * qk + 2, :],
                                                       in1=repeat_mid(sc, 2), op=ALU.mult)
                    last.then_inc(table_done, 1)

                def stage(i, d, t, k):
                    j = i + d
                    wait(pool, xs_done, 4 * (j - 1) + 4)
                    wait(pool, stage_t_full, j)
                    nc.gpsimd.tensor_copy(xin[:, :], cols(xs, (j % B) * SEQ, SEQ)).then_inc(staged, 1)

                def rotate(i, d, t, k):
                    u = 4 * (i + d) + t
                    pl = plain[:, k, :].rearrange("p (h a c) -> p h a c", h=HEADS, a=2)
                    mo = moved[:, k, :].rearrange("p (h a c) -> p h a c", h=HEADS, a=2)
                    tu = turned[:, k, :].rearrange("p (h a c) -> p h a c", h=HEADS, a=2)
                    pool.wait_ge(rope_mul, 4 * u + 2 * k + 2)
                    wait(pool, heads_t_full, 4 * (u - 1) + 2 * k + 2)
                    for a in range(2):
                        last = nc.gpsimd.tensor_tensor(out=tu[:, :, a, :], in0=pl[:, :, a, :], in1=mo[:, :, 1 - a, :],
                                                       op=ALU.add)
                    last.then_inc(pool_own, 1)
                    pool.wait_ge(ss_done, 2 * u + k + 1)
                    apart(pool)
                    nc.gpsimd.tensor_scalar(ssc[:, k, :], ss[:, k, :], 1e-24, None, ALU.max).then_inc(pool_own, 1)
                    pool.wait_ge(pool_own, 3 * (2 * u + k) + 2)
                    nc.gpsimd.tensor_tensor(out=rn[:, k, :], in0=ssc[:, k, :], in1=mhalf[:, :], op=ALU.pow).then_inc(pool_own, 1)
                    pool.wait_ge(pool_own, 3 * (2 * u + k) + 3)
                    tk = split(turned[:, k, :], DH)
                    nc.gpsimd.tensor_tensor(out=tk, in0=tk, in1=repeat_last(rn[:, k, :], DH), op=ALU.mult).then_inc(rope_done, 1)

                def add_b2(i, d, t, k):
                    j = i + d
                    u = 4 * j + t
                    pool.wait_ge(x1_done, u + 1)
                    wait(pool, xs_done, DONE_AHEAD + 4 * (j - 2) + t + 1)
                    apart(pool)
                    nc.gpsimd.tensor_tensor(out=cols(x1b, (j % 2) * SEQ + t * P, P), in0=x1[:, t * P:(t + 1) * P],
                                            in1=cols(b2b, slot_of(j) * P, P), op=ALU.add).then_inc(x1b_done, 1)

                rs_own = m.sem("rstd_own")

                def inv_std(i, d, t, k):
                    u = 4 * (i + d) + t
                    pool.wait_ge(mv_done, u + 1)
                    apart(pool)
                    nc.gpsimd.tensor_scalar(ve[:, :], mv[:, 1:2], EPS, None, ALU.add).then_inc(rs_own, 1)
                    pool.wait_ge(rs_own, u + 1)
                    wait(pool, xn_done, u)
                    nc.gpsimd.tensor_tensor(out=rstd[:, :], in0=ve[:, :], in1=mhalf[:, 0:1], op=ALU.pow).then_inc(rstd_done, 1)

                work = {"table": table, "stage": stage, "rope": rotate, "out": add_b2, "back": inv_std}
                for part, i in parts(pool):
                    for kind, d, t, k in part:
                        if kind in work:
                            work[kind](i, d, t, k)

            @block.scalar
            def _(act):
                act.wait_ge(pool_set, 7)
                act.wait_ge(b_set, 2)

                def stage_t(i, d, t, k):
                    j = i + d
                    act.wait_ge(stage_t_full, j + 1)
                    wait(act, proj_full, 24 * j)
                    nc.scalar.activation(xT[0:P // 2, 0:SEQ], bk_turn[0:P // 2, :], ACT.Copy)
                    nc.scalar.activation(xT[P // 2:P, 1:SEQ + 1], bk_turn[P // 2:P, :], ACT.Copy).then_inc(stage_t_done, 1)

                def project(i, d, t, c):
                    j = i + d
                    u = 4 * j + t
                    act.wait_ge(proj_full, 6 * u + c + 1)
                    if c < 4:
                        wait(act, ss_done, 2 * (u - 1) + c // 2 + 1)
                        nc.scalar.activation(squares[:, c // 2, (c % 2) * 512:(c % 2) * 512 + 512],
                                             bk_proj[c % 2][:, :], ACT.Square).then_inc(sq_done, 1)
                    else:
                        wait(act, pv_done, 32 * (j - 1) + min(8 * (t + 2), 32))
                        nc.scalar.activation(V[:, t, (c - 4) * 8:(c - 3) * 8, 0:DH], split(bk_proj[c % 2][:, :], DH),
                                             ACT.Copy).then_inc(v_done, 1)

                def heads_t(i, d, t, k):
                    j = i + d
                    u = 4 * j + t
                    act.wait_ge(heads_t_full, 4 * u + k + 1)
                    src = split(bk_turn[:, :], P)
                    if k < 2:
                        wait(act, s_full, 8 * (u - 1))
                        to = qT[:, t % 2, 4 * k:4 * k + 4, :, :]
                        nc.scalar.activation(to[0:DH, :, 0, :], src[0:DH], ACT.Copy)
                        nc.scalar.activation(to[DH:P, :, 1, :], src[DH:P], ACT.Copy).then_inc(heads_t_done, 1)
                    else:
                        wait(act, s_full, 32 * (j - 1) + min(8 * (t + 2), 32))
                        nc.scalar.activation(kT[:, 4 * (k - 2):4 * (k - 2) + 4, WIN + t * P:WIN + (t + 1) * P], src,
                                             ACT.Copy).then_inc(heads_t_done, 1)

                def exponent(i, d, t, p):
                    g = 8 * (4 * (i + d) + t) + p
                    lo = 0 if t else WIN
                    act.wait_ge(s_max, g + 1)
                    wait(act, pt_full, g - 1)
                    for h in range(2):
                        last = nc.scalar.activation(probs[:, p % 2, h, LEFT + lo:LEFT + KEYS],
                                                    bk_s[p % 2][:, h * KEYS + lo:(h + 1) * KEYS], ACT.Exp,
                                                    bias=nmax[:, p % 2, h:h + 1])
                    last.then_inc(s_exp, 1)

                def probs_t(i, d, t, p):
                    g = 8 * (4 * (i + d) + t) + p
                    n = 2 * P + 2 * WIN if t else 2 * P
                    act.wait_ge(pt_full, g + 1)
                    wait(act, pv_done, g - 1)
                    nc.scalar.activation(pT[:, p % 2, 0:n], bk_pT[:, 0:n], ACT.Copy).then_inc(pt_done, 1)

                def out_t(i, d, t, k):
                    u = 4 * (i + d) + t
                    act.wait_ge(out_t_full, 2 * u + k + 1)
                    wait(act, out_full, u)
                    nc.scalar.activation(OT[:, k * 512:(k + 1) * 512], bk_turn[:, :], ACT.Copy).then_inc(out_t_done, 1)

                def shift(i, d, t, k):
                    u = 4 * (i + d) + t
                    act.wait_ge(shift_full, u + 1)
                    wait(act, back_full, u)
                    nc.scalar.activation(x1T[0:P // 2, t * P:(t + 1) * P], bk_sum[0:P // 2, 0:P], ACT.Copy)
                    nc.scalar.activation(x1T[P // 2:P, t * P + 1:(t + 1) * P + 1], bk_sum[P // 2:P, 0:P],
                                         ACT.Copy).then_inc(shift_done, 1)

                def back(i, d, t, k):
                    u = 4 * (i + d) + t
                    act.wait_ge(back_full, u + 1)
                    wait(act, xn_done, u)
                    nc.scalar.activation(xb[:, :], bk_sum[:, 0:P], ACT.Copy).then_inc(back_done, 1)

                def gelu(i, d, t, k):
                    j = i + d
                    act.wait_ge(up_done, 8 * j + 8)
                    nc.scalar.activation(gate[:, :, :], gate[:, :, :], ACT.Gelu).then_inc(gelu_done, 1)

                def gate_t(i, d, t, k):
                    u = 4 * (i + d) + t
                    act.wait_ge(gate_full, u + 1)
                    wait(act, down_full, u)
                    nc.scalar.activation(hidT[:, 0:2 * P], bk_turn[:, 0:2 * P], ACT.Copy)
                    nc.scalar.activation(hidT[0:HREST, 2 * P:3 * P], bk_turn[0:HREST, 2 * P:3 * P],
                                         ACT.Copy).then_inc(gate_done, 1)

                work = {"stage_t": stage_t, "project": project, "heads_t": heads_t, "scores": exponent,
                        "probs_t": probs_t, "out_t": out_t, "shift": shift, "back": back, "gelu": gelu, "gate": gate_t}
                for part, i in parts(act):
                    for kind, d, t, k in part:
                        if kind in work:
                            work[kind](i, d, t, k)

            @block.vector
            def _(dve):
                nc.vector.tensor_copy(band[:, :], const[:, C_BAND:C_BAND + 2 * KEYS]).then_inc(b_set, 1)
                nc.vector.tensor_copy(identb[:, :], ident).then_inc(b_set, 1)
                nc.vector.memset(nmax[:, :, :], 0.0).then_inc(xs_done, DONE_AHEAD)
                nc.vector.memset(rsum[:, :, :], 0.0).then_inc(hid_done, HID_AHEAD)
                dve.wait_ge(pool_set, 7)
                dve.wait_ge(b_set, 2)
                dve.wait_ge(const_in, 16 * NC)
                dve.wait_ge(xs_done, DONE_AHEAD)
                dve.wait_ge(hid_done, HID_AHEAD)
                rsum_own, bn_own = m.sem("rsum_own"), m.sem("bn_own")

                def project(i, d, t, c):
                    if c >= 4:
                        return
                    u = 4 * (i + d) + t
                    k = c // 2
                    dve.wait_ge(proj_full, 6 * u + c + 1)
                    dve.wait_ge(sq_done, 4 * u + c + 1)
                    dve.wait_ge(table_done, u + 1)
                    wait(dve, rope_done, 2 * (u - 1) + k + 1)
                    at = slice((c % 2) * 512, (c % 2) * 512 + 512)
                    a = split(bk_proj[c % 2][:, :], DH)
                    nc.vector.tensor_tensor(split(plain[:, k, at], DH), a, repeat_mid(rope[:, t % 2, 2 * k, :], 8), ALU.mult)
                    nc.vector.tensor_tensor(split(moved[:, k, at], DH), a, repeat_mid(rope[:, t % 2, 2 * k + 1, :], 8),
                                            ALU.mult).then_inc(rope_mul, 1)

                def norms(i, d, t, k):
                    u = 4 * (i + d) + t
                    dve.wait_ge(sq_done, 4 * u + 2 * k + 2)
                    wait(dve, rope_done, 2 * (u - 1) + k + 1)
                    nc.vector.tensor_reduce(ss[:, k, :], split(squares[:, k, :], DH), AX.X, ALU.add).then_inc(ss_done, 1)

                def row_max(i, d, t, p):
                    g = 8 * (4 * (i + d) + t) + p
                    lo = 0 if t else WIN
                    dve.wait_ge(s_full, g + 1)
                    wait(dve, s_exp, g - 1)
                    nc.vector.tensor_reduce(nmax[:, p % 2, :], split(bk_s[p % 2][:, 0:2 * KEYS], KEYS)[:, :, lo:KEYS],
                                            AX.X, ALU.max, negate=True).then_inc(s_max, 1)

                def attended(i, d, t, p):
                    if p % 2 == 0:
                        return
                    u = 4 * (i + d) + t
                    q = p // 2
                    G = 4 * u + q
                    o = bk_o[:, 0:4 * (DH + 1)].rearrange("p (h c) -> p h c", c=DH + 1)
                    dve.wait_ge(pv_done, 8 * u + p + 1)
                    wait(dve, o_done, G)
                    nc.vector.reciprocal(rsum[:, q % 2, :], o[:, :, DH]).then_inc(rsum_own, 1)
                    dve.wait_ge(rsum_own, G + 1)
                    wait(dve, out_t_full, 2 * (u - 1) + q // 2 + 1)
                    nc.vector.tensor_tensor(split(O[:, q * 256:(q + 1) * 256], DH), o[:, :, 0:DH],
                                            repeat_last(rsum[:, q % 2, :], DH), ALU.mult).then_inc(o_done, 1)

                def residual(i, d, t, k):
                    j = i + d
                    u = 4 * j + t
                    dve.wait_ge(out_full, u + 1)
                    wait(dve, x1b_done, 4 * (j - 1) + t + 1)
                    wait(dve, xs_done, DONE_AHEAD + 4 * (j - 4) + t + 1)
                    wait(dve, shift_full, 4 * (j - 1) + t + 1)
                    nc.vector.tensor_tensor(x1[:, t * P:(t + 1) * P], bk_sum[:, 0:P], cols(xs, tile_at(j, t), P),
                                            ALU.add).then_inc(x1_done, 1)

                def stats(i, d, t, k):
                    u = 4 * (i + d) + t
                    dve.wait_ge(back_done, u + 1)
                    wait(dve, mv_done, u)
                    nc.vector.bn_stats(st[:, :], xb[:, :]).then_inc(bn_own, 1)
                    dve.wait_ge(bn_own, u + 1)
                    wait(dve, rstd_done, u)
                    wait(dve, xn_done, u)
                    apart(dve)
                    nc.vector.bn_aggr(mv[:, :], st[:, :]).then_inc(mv_done, 1)

                def normalise(i, d, t, k):
                    u = 4 * (i + d) + t
                    dve.wait_ge(rstd_done, u + 1)
                    wait(dve, norm_t_full, u)
                    nc.vector.tensor_scalar(xn[:, :], xb[:, :], mv[:, 0:1], rstd[:, :], ALU.subtract, ALU.mult).then_inc(xn_done, 1)

                def norm_t(i, d, t, k):
                    j = i + d
                    u = 4 * j + t
                    l = layer_of(j)
                    dve.wait_ge(norm_t_full, u + 1)
                    wait(dve, up_full, 2 * u)
                    nc.vector.tensor_scalar(xnT[:, :], bk_sum[:, 0:P], cols(lng, l, 1), cols(lnb, l, 1),
                                            ALU.mult, ALU.add).then_inc(norm_t_done, 1)

                def up(i, d, t, k):
                    j = i + d
                    u = 4 * j + t
                    dve.wait_ge(up_full, 2 * u + k + 1)
                    dve.wait_ge(hid_done, HID_AHEAD + 4 * (j - 1) + t + 1)
                    nc.vector.tensor_tensor((lin, gate)[k][:, t, :], bk_proj[k][:, 0:HID],
                                            cols(b1b, slot_of(j) * 2 * HID + k * HID, HID), ALU.add).then_inc(up_done, 1)

                def hidden(i, d, t, k):
                    j = i + d
                    u = 4 * j + t
                    dve.wait_ge(gelu_done, j + 1)
                    wait(dve, gate_full, u - 1 if t else u)
                    nc.vector.tensor_tensor(hid[:, t % 2, :], lin[:, t, :], gate[:, t, :], ALU.mult).then_inc(hid_done, 1)

                def down(i, d, t, k):
                    j = i + d
                    u = 4 * j + t
                    dve.wait_ge(down_full, u + 1)
                    dve.wait_ge(x1b_done, u + 1)
                    dve.wait_ge(staged, j + 1)
                    nc.vector.tensor_tensor(cols(xs, tile_at(j, t), P), bk_sum[:, 0:P], cols(x1b, (j % 2) * SEQ + t * P, P),
                                            ALU.add).then_inc(xs_done, 1)

                work = {"project": project, "rope": norms, "scores": row_max, "pv": attended, "out": residual,
                        "back": stats, "norm": normalise, "norm_t": norm_t, "up": up, "hidden": hidden, "down": down}
                for part, i in parts(dve):
                    for kind, d, t, k in part:
                        if kind in work:
                            work[kind](i, d, t, k)

            @block.tensor
            def _(pe):
                pe.wait_ge(pool_set, 7)
                pe.wait_ge(b_set, 2)

                def stage_t(i, d, t, k):
                    pe.wait_ge(staged, i + d + 1)
                    for n in range(TILES):
                        last = nc.tensor.transpose(bk_turn[:, n * P:(n + 1) * P], xin[:, n * P:(n + 1) * P], ident)
                    last.then_inc(stage_t_full, 1)

                def project(i, d, t, c):
                    j = i + d
                    if c == 0:
                        pe.wait_ge(stage_t_done, j + 1)
                        pe.wait_ge(w_in, (layer_of(j) + 1) * NW * 16)
                    nc.tensor.matmul(bk_proj[c % 2][:, :], xT[:, t * P:(t + 1) * P],
                                     cols(wts, slot_of(j) * W_ALL + W_QKV + c * 512, 512),
                                     start=True, stop=True).then_inc(proj_full, 1)

                def heads_t(i, d, t, k):
                    u = 4 * (i + d) + t
                    pe.wait_ge(rope_done, 2 * u + k // 2 + 1)
                    for n in range(4):
                        at = ((k % 2) * 4 + n) * P
                        last = nc.tensor.transpose(bk_turn[:, n * P:(n + 1) * P], turned[:, k // 2, at:at + P], ident)
                    last.then_inc(heads_t_full, 1)

                def scores(i, d, t, p):
                    g = 8 * (4 * (i + d) + t) + p
                    lo = 0 if t else WIN
                    if p == 0:
                        pe.wait_ge(heads_t_done, 4 * (4 * (i + d) + t) + 4)
                    wait(pe, s_exp, g - 1)
                    out = split(bk_s[p % 2][:, 0:2 * KEYS], KEYS)
                    nc.tensor.matmul(out[:, :, lo:KEYS], identb[:, :], split(band[:, :], KEYS)[:, :, lo:KEYS],
                                     start=True, stop=False, skip_group_check=True)
                    for h in range(2):
                        last = nc.tensor.matmul(out[:, h, lo:KEYS], qT[:, t % 2, p, h, :],
                                                kT[:, p, t * P + lo:t * P + KEYS], start=False, stop=True,
                                                skip_group_check=True)
                    last.then_inc(s_full, 1)

                def probs_t(i, d, t, p):
                    g = 8 * (4 * (i + d) + t) + p
                    pe.wait_ge(s_exp, g + 1)
                    wait(pe, pt_done, g)
                    for h in range(2):
                        last = nc.tensor.transpose(bk_pT[:, h * P:(h + 1) * P], probs[:, p % 2, h, LEFT + WIN:LEFT + KEYS], ident)
                    if t:
                        for h in range(2):
                            last = nc.tensor.transpose(bk_pT[:, 2 * P + h * WIN:2 * P + (h + 1) * WIN],
                                                       probs[0:WIN, p % 2, h, 0:P], ident[0:WIN, 0:WIN])
                    last.then_inc(pt_full, 1)

                def pv(i, d, t, p):
                    u = 4 * (i + d) + t
                    g = 8 * u + p
                    pe.wait_ge(pt_done, g + 1)
                    if p == 0:
                        pe.wait_ge(v_done, 2 * u + 2)
                    if p % 2 == 0:
                        wait(pe, o_done, 4 * u + p // 2)
                    for h in range(2):
                        at = ((p % 2) * 2 + h) * (DH + 1)
                        last = nc.tensor.matmul(bk_o[:, at:at + DH + 1], pT[:, p % 2, h * P:(h + 1) * P],
                                                V[:, t, 2 * p + h, :], start=True, stop=(t == 0), skip_group_check=True)
                        if t:
                            last = nc.tensor.matmul(bk_o[0:WIN, at:at + DH + 1],
                                                    pT[:, p % 2, 2 * P + h * WIN:2 * P + (h + 1) * WIN],
                                                    V[:, t - 1, 2 * p + h, :], start=False, stop=True, skip_group_check=True)
                    last.then_inc(pv_done, 1)

                def out_t(i, d, t, k):
                    u = 4 * (i + d) + t
                    pe.wait_ge(o_done, 4 * u + 2 * k + 2)
                    for n in range(4):
                        at = (k * 4 + n) * P
                        last = nc.tensor.transpose(bk_turn[:, n * P:(n + 1) * P], O[:, at:at + P], ident)
                    last.then_inc(out_t_full, 1)

                def out(i, d, t, k):
                    j = i + d
                    pe.wait_ge(out_t_done, 2 * (4 * j + t) + 2)
                    for n in range(PAIRS):
                        last = nc.tensor.matmul(bk_sum[:, 0:P], OT[:, n * P:(n + 1) * P],
                                                cols(wts, slot_of(j) * W_ALL + W_O + n * P, P),
                                                start=(n == 0), stop=(n == PAIRS - 1))
                    last.then_inc(out_full, 1)

                def shift(i, d, t, k):
                    pe.wait_ge(x1_done, 4 * (i + d) + t + 1)
                    nc.tensor.transpose(bk_sum[:, 0:P], x1[:, t * P:(t + 1) * P], ident).then_inc(shift_full, 1)

                def back(i, d, t, k):
                    pe.wait_ge(shift_done, 4 * (i + d) + t + 1)
                    nc.tensor.transpose(bk_sum[:, 0:P], x1T[:, t * P:(t + 1) * P], ident).then_inc(back_full, 1)

                def norm_t(i, d, t, k):
                    pe.wait_ge(xn_done, 4 * (i + d) + t + 1)
                    nc.tensor.transpose(bk_sum[:, 0:P], xn[:, :], ident).then_inc(norm_t_full, 1)

                def up(i, d, t, k):
                    j = i + d
                    pe.wait_ge(norm_t_done, 4 * j + t + 1)
                    nc.tensor.matmul(bk_proj[k][:, 0:HID], xnT[:, :],
                                     cols(wts, slot_of(j) * W_ALL + W_UP + k * HID, HID), start=True, stop=True).then_inc(up_full, 1)

                def gate_t(i, d, t, k):
                    pe.wait_ge(hid_done, HID_AHEAD + 4 * (i + d) + t + 1)
                    for n in range(HCH):
                        w = min(P, HID - n * P)
                        last = nc.tensor.transpose(bk_turn[0:w, n * P:(n + 1) * P], hid[:, t % 2, n * P:n * P + w], ident)
                    last.then_inc(gate_full, 1)

                def down(i, d, t, k):
                    j = i + d
                    pe.wait_ge(gate_done, 4 * j + t + 1)
                    for n in range(HCH):
                        w = min(P, HID - n * P)
                        last = nc.tensor.matmul(bk_sum[:, 0:P], hidT[0:w, n * P:(n + 1) * P],
                                                wts[0:w, bass.ds(slot_of(j) * W_ALL + W_DOWN + n * P, P)],
                                                start=(n == 0), stop=(n == HCH - 1))
                    last.then_inc(down_full, 1)

                work = {"stage_t": stage_t, "project": project, "heads_t": heads_t, "scores": scores,
                        "probs_t": probs_t, "pv": pv, "out_t": out_t, "out": out, "shift": shift, "back": back,
                        "norm_t": norm_t, "up": up, "gate": gate_t, "down": down}
                for part, i in parts(pe):
                    for n, (kind, d, t, k) in enumerate(part):
                        for bank, uses in BANK_STEPS.items():
                            if uses((kind, d, t, k)):
                                before = bank_before(part, n, bank)
                                if before:
                                    for sem, value in emptied(before[0], i - before[1]):
                                        wait(pe, sem, value)
                        if kind in work:
                            work[kind](i, d, t, k)


def gathered_attention(nc, const, X, XS, ctx_h, Wq, Wkv, Wc):
    with ExitStack() as es:
        m = Memory(nc, es, "c")
        xv, sv = X[:, :], XS[:, :]
        wq = m.sb("wq", [P, P])
        wc = m.sb("wc", [P, P])
        wkv = m.sb("wkv", [2 * XDH, P])
        wqT = m.sb("wq_t", [P, P])
        wcT = m.sb("wc_t", [P, P])
        wkT = m.sb("wk_t", [P, XHEADS, XDH])
        wvT = m.sb("wv_t", [P, XDH])
        cb = m.sb("ctx", [CTX, P])
        cT = m.sb("ctx_t", [P, CTX])
        st = m.sb("stats", [P, TILES, 6])
        mv = m.sb("mean_var", [P, TILES, 2])
        ve = m.sb("var_eps", [P, TILES])
        rs = m.sb("rstd", [P, TILES])
        mhalf = m.sb("minus_half", [P, TILES])
        z = m.sb("normed", [P, TILES, P])
        zT = m.sb("normed_t", [P, SEQ])
        qpT = m.sb("queries_t", [P, SEQ])
        sc = m.sb("scores", [P, TILES, CTX])
        top = m.sb("top", [P, TILES, 8])
        pick = m.sb("pick", [P, TILES, 8], u32)
        pickf = m.sb("pick_f", [P, TILES])
        one = m.sb("onehot", [P, TILES, CTX])
        pres = m.sb("present", [P, CTX])
        absent = m.sb("absent", [P, CTX])
        mk = m.sb("keys", [P, CTX])
        mks = m.sb("key_first_terms", [P, CTX])
        mk0 = m.sb("key_first", [P, 1])
        mkp = m.sb("keys_present", [P, CTX])
        mkd = m.sb("keys_used", [P, CTX])
        kbd = m.sb("keys_by_head", [P, XHEADS, CTX])
        cnt = m.sb("counts", [CTX, 1])
        v9 = m.sb("values", [CTX, XDH + 1])
        nm = m.sb("neg_max", [P, XHEADS])
        lg = m.sb("logits", [P, XHEADS, CTX])
        pr = m.sb("probs", [P, XHEADS, CTX])
        pT = m.sb("probs_t", [CTX, 4, 512])
        ri = m.sb("inv_sum", [P, XHEADS])
        o = m.sb("attended", [P, P])
        oT = m.sb("attended_t", [P, P])
        bk_lg = [m.bank(f"logits{n}") for n in range(3)]
        bk_t = [m.bank("turned0"), m.bank("turned1")]
        bk_a, bk_b, bk_o = m.bank("work0"), m.bank("work1"), m.bank("attended")
        GROUPS = [(0, 6), (6, 6), (12, 4)]

        names = ("w_in", "ctx_in", "half_set", "wT_full", "wT_done", "x_done", "st_done", "stats_", "ve_done", "rstd_", "normed_",
                 "zt_full", "zt_done", "ct_full", "ct_done", "q_full", "q_done", "s_full", "s_done", "top_done",
                 "pick_done", "pickf_done", "one_done", "cnt_full", "mk_full", "pres_done", "absent_done", "mk_done",
                 "mks_done", "mk0_done", "mkp_done", "mkd_done", "kbd_done", "cnt_done", "v_done", "lg_full", "lmax_done", "lsub_done",
                 "exp_done", "pt_full", "pt_done", "o_full", "ri_done", "o_done", "ot_full", "ot_done", "y_full", "y_done")
        (w_in, ctx_in, half_set, wT_full, wT_done, x_done, st_done, stats, ve_done, rstd, normed, zT_full, zT_done, cT_full, cT_done,
         q_full, q_done, s_full, s_done, top_done, pick_done, pickf_done, one_done, cnt_full, mk_full, pres_done, absent_done,
         mk_done, mks_done, mk0_done, mkp_done, mkd_done, kbd_done, cnt_done, v_done, lg_full, lmax_done, lsub_done, exp_done,
         pT_full, pT_done, o_full, ri_done, o_done, oT_full, oT_done, y_full, y_done) = [m.sem(n) for n in names]
        ident = const[:, C_IDENT:C_IDENT + P]
        ones = const[:, C_ONES:C_ONES + P]
        row0 = const[:, C_ROW0:C_ROW0 + P]

        with nc.Block() as block:
            @block.sync
            def _(sp):
                sp.dma_start(wq[:, :], Wq).then_inc(w_in, 16)
                sp.dma_start(wc[:, :], Wc).then_inc(w_in, 16)
                sp.dma_start(wkv[:, :], Wkv).then_inc(w_in, 16)
                with sp.Fori(0, B) as b:
                    sp.wait_ge(cT_full, b)
                    sp.dma_start(cb[:, :], ctx_h[bass.ds(b, 1), :, :].rearrange("o j d -> (o j) d")).then_inc(ctx_in, 16)

            @block.gpsimd
            def _(pool):
                nc.gpsimd.memset(mhalf[:, :], -0.5).then_inc(half_set, 1)
                pool.wait_ge(half_set, 1)
                with pool.Fori(0, B) as b:
                    pool.wait_ge(stats, b + 1)
                    apart(pool)
                    nc.gpsimd.tensor_scalar(ve[:, :], mv[:, :, 1], EPS, None, ALU.add).then_inc(ve_done, 1)
                    pool.wait_ge(ve_done, b + 1)
                    pool.wait_ge(normed, b)
                    nc.gpsimd.tensor_tensor(out=rs[:, :], in0=ve[:, :], in1=mhalf[:, :], op=ALU.pow).then_inc(rstd, 1)

            @block.scalar
            def _(act):
                act.wait_ge(wT_full, 1)
                nc.scalar.activation(wqT[:, :], bk_a[:, 0:P], ACT.Copy)
                nc.scalar.activation(wcT[:, :], bk_a[:, P:2 * P], ACT.Copy)
                nc.scalar.activation(wvT[:, :], bk_a[:, 2 * P + XDH:2 * P + 2 * XDH], ACT.Copy)
                nc.scalar.activation(wkT[:, :, :], repeat_mid(bk_a[:, 2 * P:2 * P + XDH], XHEADS), ACT.Copy).then_inc(wT_done, 1)
                with act.Fori(0, B) as b:
                    act.wait_ge(cT_full, b + 1)
                    act.wait_ge(mk_full, b)
                    nc.scalar.activation(cT[:, :], bk_b[:, 0:CTX], ACT.Copy).then_inc(cT_done, 1)
                    act.wait_ge(zT_full, b + 1)
                    act.wait_ge(q_full, b)
                    nc.scalar.activation(zT[:, :], bk_a[:, :], ACT.Copy).then_inc(zT_done, 1)
                    act.wait_ge(q_full, b + 1)
                    act.wait_ge(lg_full, b * TILES)
                    nc.scalar.activation(qpT[:, :], bk_b[:, :], ACT.Copy).then_inc(q_done, 1)
                    act.wait_ge(s_full, b + 1)
                    act.wait_ge(one_done, b)
                    nc.scalar.activation(sc[:, :, :], split(bk_a[:, 0:TILES * CTX], CTX), ACT.Copy).then_inc(s_done, 1)

                    def attended_t(t):
                        u = b * TILES + t
                        act.wait_ge(oT_full, u + 1)
                        act.wait_ge(y_full, u)
                        nc.scalar.activation(oT[:, :], bk_b[:, 0:P], ACT.Copy).then_inc(oT_done, 1)

                    for t in range(TILES):
                        u = b * TILES + t
                        act.wait_ge(lsub_done, u + 1)
                        act.wait_ge(pT_full, 4 * u)
                        nc.scalar.activation(pr[:, :, :], lg[:, :, :], ACT.Exp).then_inc(exp_done, 1)
                        for q in range(4):
                            act.wait_ge(pT_full, 4 * u + q + 1)
                            if q == 0:
                                act.wait_ge(o_full, u)
                            nc.scalar.activation(pT[:, q, :], bk_t[q % 2][0:CTX, :], ACT.Copy).then_inc(pT_done, 1)
                            if q == 1 and t:
                                attended_t(t - 1)
                    attended_t(TILES - 1)

            @block.vector
            def _(dve):
                with dve.Fori(0, B) as b:
                    xb, sb_ = cols(xv, b * SEQ, SEQ), cols(sv, b * SEQ, SEQ)
                    nc.vector.tensor_tensor(xb, xb, sb_, ALU.add).then_inc(x_done, 1)
                    dve.wait_ge(x_done, b + 1)
                    apart(dve)
                    for t in range(TILES):
                        last = nc.vector.bn_stats(st[:, t, :], cols(xv, b * SEQ + t * P, P))
                    last.then_inc(st_done, 1)
                    dve.wait_ge(st_done, b + 1)
                    apart(dve)
                    for t in range(TILES):
                        last = nc.vector.bn_aggr(mv[:, t, :], st[:, t, :])
                    last.then_inc(stats, 1)
                    dve.wait_ge(rstd, b + 1)
                    dve.wait_ge(stats, b + 1)
                    for t in range(TILES):
                        last = nc.vector.tensor_scalar(z[:, t, :], cols(xv, b * SEQ + t * P, P), mv[:, t, 0:1],
                                                       rs[:, t:t + 1], ALU.subtract, ALU.mult)
                    last.then_inc(normed, 1)
                    dve.wait_ge(s_done, b + 1)
                    apart(dve)
                    for t in range(TILES):
                        last = nc.vector.max(top[:, t, :], sc[:, t, :])
                    last.then_inc(top_done, 1)
                    dve.wait_ge(top_done, b + 1)
                    apart(dve)
                    for t in range(TILES):
                        last = nc.vector.max_index(pick[:, t, :], top[:, t, :], sc[:, t, :])
                    last.then_inc(pick_done, 1)
                    dve.wait_ge(pick_done, b + 1)
                    nc.vector.tensor_copy(pickf[:, :], pick[:, :, 0]).then_inc(pickf_done, 1)
                    dve.wait_ge(pickf_done, b + 1)
                    dve.wait_ge(cnt_full, b)
                    for t in range(TILES):
                        last = nc.vector.tensor_scalar(one[:, t, :], const[:, C_IOTA:C_IOTA + CTX], pickf[:, t:t + 1],
                                                       None, ALU.is_equal)
                    last.then_inc(one_done, 1)
                    dve.wait_ge(cnt_full, b + 1)
                    dve.wait_ge(mk_full, b + 1)
                    nc.vector.tensor_scalar(pres[:, :], bk_a[:, 0:CTX], 0.5, None, ALU.is_gt).then_inc(pres_done, 1)
                    nc.vector.tensor_scalar(absent[:, :], bk_a[:, 0:CTX], 0.5, None, ALU.is_lt).then_inc(absent_done, 1)
                    nc.vector.tensor_scalar(mk[:, :], bk_b[:, 0:CTX], float(np.float32(1.0) / np.sqrt(XDH).astype(np.float32)), None, ALU.mult).then_inc(mk_done, 1)
                    nc.vector.tensor_copy(cnt[:, :], bk_a[0:CTX, 2 * CTX:2 * CTX + 1]).then_inc(cnt_done, 1)
                    dve.wait_ge(mk_done, b + 1)
                    nc.vector.tensor_tensor(mks[:, :], bk_a[:, CTX:2 * CTX], mk[:, :], ALU.mult).then_inc(mks_done, 1)
                    nc.vector.tensor_tensor(mkp[:, :], mk[:, :], pres[:, :], ALU.mult).then_inc(mkp_done, 1)
                    dve.wait_ge(mks_done, b + 1)
                    nc.vector.tensor_reduce(mk0[:, :], mks[:, :], AX.X, ALU.add).then_inc(mk0_done, 1)
                    dve.wait_ge(mk0_done, b + 1)
                    dve.wait_ge(mkp_done, b + 1)
                    nc.vector.scalar_tensor_tensor(mkd[:, :], absent[:, :], mk0[:, :], mkp[:, :], ALU.mult, ALU.add).then_inc(mkd_done, 1)
                    dve.wait_ge(mkd_done, b + 1)
                    dve.wait_ge(lg_full, b * TILES)
                    nc.vector.tensor_tensor(kbd[:, :, :], repeat_mid(mkd[:, :], XHEADS),
                                            repeat_last(const[:, C_HEADS:C_HEADS + XHEADS], CTX), ALU.mult).then_inc(kbd_done, 1)
                    dve.wait_ge(cnt_done, b + 1)
                    dve.wait_ge(o_full, b * TILES)
                    nc.vector.tensor_scalar(v9[:, 0:XDH], bk_b[0:CTX, CTX:CTX + XDH], cnt[:, :], None, ALU.mult)
                    nc.vector.tensor_copy(v9[:, XDH:XDH + 1], cnt[:, :]).then_inc(v_done, 1)

                    def stable(t):
                        u = b * TILES + t
                        dve.wait_ge(lg_full, u + 1)
                        dve.wait_ge(lsub_done, u)
                        for (h, n), bank in zip(GROUPS, bk_lg):
                            last = nc.vector.tensor_reduce(nm[:, h:h + n], split(bank[:, 0:n * CTX], CTX), AX.X, ALU.max)
                        last.then_inc(lmax_done, 1)
                        dve.wait_ge(lmax_done, u + 1)
                        dve.wait_ge(exp_done, u)
                        for (h, n), bank in zip(GROUPS, bk_lg):
                            last = nc.vector.tensor_tensor(lg[:, h:h + n, :], split(bank[:, 0:n * CTX], CTX),
                                                           repeat_last(nm[:, h:h + n], CTX), ALU.subtract)
                        last.then_inc(lsub_done, 1)

                    def residual(t):
                        u = b * TILES + t
                        dve.wait_ge(y_full, u + 1)
                        xt = cols(xv, b * SEQ + t * P, P)
                        nc.vector.tensor_tensor(xt, bk_a[:, 0:P], xt, ALU.add).then_inc(y_done, 1)

                    stable(0)
                    for t in range(TILES):
                        u = b * TILES + t
                        if t + 1 < TILES:
                            stable(t + 1)
                        if t:
                            residual(t - 1)
                        ob = split(bk_o[:, 0:XHEADS * (XDH + 1)], XDH + 1)
                        dve.wait_ge(o_full, u + 1)
                        dve.wait_ge(o_done, u)
                        nc.vector.reciprocal(ri[:, :], ob[:, :, XDH]).then_inc(ri_done, 1)
                        dve.wait_ge(ri_done, u + 1)
                        dve.wait_ge(oT_full, u)
                        nc.vector.tensor_tensor(split(o[:, :], XDH), ob[:, :, 0:XDH], repeat_last(ri[:, :], XDH),
                                                ALU.mult).then_inc(o_done, 1)
                    residual(TILES - 1)

            @block.tensor
            def _(pe):
                pe.wait_ge(w_in, 48)
                nc.tensor.transpose(bk_a[:, 0:P], wq[:, :], ident)
                nc.tensor.transpose(bk_a[:, P:2 * P], wc[:, :], ident)
                nc.tensor.transpose(bk_a[:, 2 * P:2 * P + 2 * XDH], wkv[:, :], ident[0:2 * XDH, 0:2 * XDH]).then_inc(wT_full, 1)
                pe.wait_ge(wT_done, 1)
                with pe.Fori(0, B) as b:
                    pe.wait_ge(ctx_in, 16 * b + 16)
                    pe.wait_ge(oT_done, b * TILES)
                    nc.tensor.transpose(bk_b[:, 0:CTX], cb[:, :], ident[0:CTX, 0:CTX]).then_inc(cT_full, 1)
                    pe.wait_ge(normed, b + 1)
                    pe.wait_ge(y_done, b * TILES)
                    for t in range(TILES):
                        last = nc.tensor.transpose(bk_a[:, t * P:(t + 1) * P], z[:, t, :], ident)
                    last.then_inc(zT_full, 1)
                    pe.wait_ge(zT_done, b + 1)
                    pe.wait_ge(cT_done, b + 1)
                    nc.tensor.matmul(bk_b[:, :], wqT[:, :], zT[:, :], start=True, stop=True).then_inc(q_full, 1)
                    pe.wait_ge(q_done, b + 1)
                    for t in range(TILES):
                        last = nc.tensor.matmul(bk_a[:, t * CTX:(t + 1) * CTX], qpT[:, t * P:(t + 1) * P], cT[:, :],
                                                start=True, stop=True)
                    last.then_inc(s_full, 1)
                    nc.tensor.matmul(bk_b[:, 0:CTX], wkT[:, :, :], cT[:, :], start=True, stop=True)
                    nc.tensor.matmul(bk_b[0:CTX, CTX:CTX + XDH], cT[:, :], wvT[:, :], start=True, stop=True).then_inc(mk_full, 1)
                    pe.wait_ge(one_done, b + 1)
                    for t in range(TILES):
                        nc.tensor.matmul(bk_a[:, 0:CTX], ones, one[:, t, :], start=(t == 0), stop=(t == TILES - 1))
                    nc.tensor.matmul(bk_a[:, CTX:2 * CTX], row0, one[:, 0, :], start=True, stop=True)
                    for t in range(TILES):
                        last = nc.tensor.matmul(bk_a[0:CTX, 2 * CTX:2 * CTX + 1], one[:, t, :], ones[:, 0:1],
                                                start=(t == 0), stop=(t == TILES - 1))
                    last.then_inc(cnt_full, 1)
                    pe.wait_ge(kbd_done, b + 1)
                    pe.wait_ge(v_done, b + 1)

                    def logits(t):
                        pe.wait_ge(lsub_done, b * TILES + t)
                        for (h, n), bank in zip(GROUPS, bk_lg):
                            last = nc.tensor.matmul(split(bank[:, 0:n * CTX], CTX), qpT[:, t * P:(t + 1) * P], kbd[:, h:h + n, :],
                                                    start=True, stop=True)
                        last.then_inc(lg_full, 1)

                    def attended_t(t):
                        u = b * TILES + t
                        pe.wait_ge(o_done, u + 1)
                        pe.wait_ge(oT_done, u)
                        nc.tensor.transpose(bk_b[:, 0:P], o[:, :], ident).then_inc(oT_full, 1)

                    def out(t):
                        u = b * TILES + t
                        pe.wait_ge(oT_done, u + 1)
                        pe.wait_ge(y_done, u)
                        nc.tensor.matmul(bk_a[:, 0:P], oT[:, :], wcT[:, :], start=True, stop=True).then_inc(y_full, 1)

                    logits(0)
                    for t in range(TILES):
                        u = b * TILES + t
                        if t + 1 < TILES:
                            logits(t + 1)
                        pe.wait_ge(exp_done, u + 1)
                        for q in range(4):
                            if q >= 2:
                                pe.wait_ge(pT_done, 4 * u + q - 1)
                            else:
                                pe.wait_ge(pT_done, 4 * u)
                            for n in range(4):
                                last = nc.tensor.transpose(bk_t[q % 2][0:CTX, n * P:(n + 1) * P], pr[:, 4 * q + n, :], ident)
                            last.then_inc(pT_full, 1)
                            if q == 1 and t:
                                attended_t(t - 1)
                        if t:
                            out(t - 1)
                        pe.wait_ge(pT_done, 4 * u + 4)
                        pe.wait_ge(o_done, u)
                        for h in range(XHEADS):
                            last = nc.tensor.matmul(bk_o[:, h * (XDH + 1):(h + 1) * (XDH + 1)],
                                                    pT[:, h // 4, (h % 4) * P:(h % 4 + 1) * P], v9[:, :], start=True, stop=True)
                        last.then_inc(o_full, 1)
                    attended_t(TILES - 1)
                    out(TILES - 1)


def mixture(nc, const, X, XS, cent, ln_g, ln_b, w1, b1, w2, b2, out_h):
    with ExitStack() as es:
        m = Memory(nc, es, "d")
        xv, zv = X[:, :], XS[:, :]
        gb = m.sb("ln_g", [EXPERTS, P])
        bb = m.sb("ln_b", [EXPERTS, P])
        b2s = m.sb("b2", [EXPERTS, P])
        cen = m.sb("centroids", [EXPERTS, P])
        cenT = m.sb("centroids_t", [P, EXPERTS])
        b1c = m.sb("b1", [P, EXPERTS * FCH])
        w1s = m.sb("w1", [P, 2, FF])
        w2s = m.sb("w2", [P, 2, FCH, P])
        st = m.sb("stats", [P, TILES, 6])
        mv = m.sb("mean_var", [P, TILES, 2])
        ve = m.sb("var_eps", [P, TILES])
        rs = m.sb("rstd", [P, TILES])
        st2 = m.sb("stats2", [P, TILES, 6])
        mv2 = m.sb("mean_var2", [P, TILES, 2])
        ve2 = m.sb("var_eps2", [P, TILES])
        rs2 = m.sb("rstd2", [P, TILES])
        mhalf = m.sb("minus_half", [P, TILES])
        zb = m.sb("z", [P, TILES, P])
        zT = m.sb("z_t", [P, SEQ])
        xn = m.sb("normed", [P, TILES, P])
        xnT = m.sb("normed_t", [P, SEQ])
        gx = m.sb("scaled", [P, SEQ])
        top = m.sb("top", [P, TILES, 8])
        aff = m.sb("affinity", [P, TILES, EXPERTS])
        pick = m.sb("pick", [P, TILES, 8], u32)
        pickf = m.sb("pick_f", [P, TILES])
        one = m.sb("onehot", [P, NT * EXPERTS])
        oneb = m.sb("onehot_now", [P, TILES, EXPERTS])
        oneT = m.sb("onehot_t", [EXPERTS, SEQ])
        ex = m.sb("exp", [P, TILES])
        ex1 = m.sb("exp1", [P, TILES])
        alpha = m.sb("alpha", [P, NT])
        xl = m.sb("expert_in", [P, NT * P])
        acc = m.sb("expert_out", [P, NT * P])
        hT = m.sb("hidden_t", [P, 2, FCH, SEQ])
        fin = m.sb("gated", [P, NT * P])

        names = ("w_in", "e_in0", "e_in1", "half_set", "cen_full", "cen_done", "st_done", "stats_", "ve_done", "rstd_",
                 "z_done", "st2_done", "stats2_", "ve2_done", "rstd2_", "xn_done", "zt_full", "zt_done", "aff_full",
                 "aff_done", "top_done", "pick_done", "pickf_done", "one_done", "exp_done", "exp1_done", "alpha_done", "onet_full", "onet_done",
                 "xnt_full", "xnt_done", "g_full", "gx_done", "xl_done", "b2_full", "acc_done", "h_full", "h_done",
                 "y_full", "y_done", "gated_done", "out_done", "stored")
        (w_in, e_in0, e_in1, half_set, cen_full, cen_done, st_done, stats, ve_done, rstd, z_done, st2_done, stats2, ve2_done,
         rstd2, xn_done, zT_full, zT_done, aff_full, aff_done, top_done, pick_done, pickf_done, one_done, exp_done, exp1_done,
         alpha_done, oneT_full, oneT_done, xnT_full, xnT_done, g_full, gx_done, xl_done, b2_full, acc_done, h_full, h_done,
         y_full, y_done, gated_done, out_done, stored) = [m.sem(n) for n in names]
        e_in = [e_in0, e_in1]
        ident = const[:, C_IDENT:C_IDENT + P]

        with ExitStack() as banks:
            mb = Memory(nc, banks, "d1")
            bk_z, bk_a, bk_x, bk_g, bk_b, bk_o, bk_y = [mb.bank(n) for n in ("z", "aff", "xn", "g", "b", "one", "y")]
            with nc.Block() as block:
                @block.sync
                def _(sp):
                    sp.dma_start(gb[:, :], ln_g).then_inc(w_in, 16)
                    sp.dma_start(bb[:, :], ln_b).then_inc(w_in, 16)
                    sp.dma_start(b2s[:, :], b2).then_inc(w_in, 16)
                    sp.dma_start(cen[:, :], cent).then_inc(w_in, 16)
                    with nc.allow_non_contiguous_dma(reason="one column per chunk of an expert"):
                        sp.dma_start(b1c[:, :], b1.rearrange("e (f p) -> p (e f)", p=P)).then_inc(w_in, 16)

                @block.gpsimd
                def _(pool):
                    nc.gpsimd.memset(mhalf[:, :], -0.5).then_inc(half_set, 1)
                    pool.wait_ge(half_set, 1)
                    with pool.Fori(0, B) as b:
                        pool.wait_ge(stats, b + 1)
                        apart(pool)
                        nc.gpsimd.tensor_scalar(ve[:, :], mv[:, :, 1], EPS, None, ALU.add).then_inc(ve_done, 1)
                        pool.wait_ge(ve_done, b + 1)
                        nc.gpsimd.tensor_tensor(out=rs[:, :], in0=ve[:, :], in1=mhalf[:, :], op=ALU.pow).then_inc(rstd, 1)
                        pool.wait_ge(stats2, b + 1)
                        apart(pool)
                        nc.gpsimd.tensor_scalar(ve2[:, :], mv2[:, :, 1], EPS, None, ALU.add).then_inc(ve2_done, 1)
                        pool.wait_ge(ve2_done, b + 1)
                        nc.gpsimd.tensor_tensor(out=rs2[:, :], in0=ve2[:, :], in1=mhalf[:, :], op=ALU.pow).then_inc(rstd2, 1)

                @block.scalar
                def _(act):
                    act.wait_ge(cen_full, 1)
                    nc.scalar.activation(cenT[:, :], bk_a[:, 0:EXPERTS], ACT.Copy).then_inc(cen_done, 1)
                    with act.Fori(0, B) as b:
                        act.wait_ge(zT_full, b + 1)
                        act.wait_ge(aff_full, b)
                        nc.scalar.activation(zT[:, :], bk_z[:, :], ACT.Copy).then_inc(zT_done, 1)
                        act.wait_ge(aff_full, b + 1)
                        act.wait_ge(one_done, b)
                        nc.scalar.activation(aff[:, :, :], split(bk_a[:, 0:TILES * EXPERTS], EXPERTS), ACT.Copy).then_inc(aff_done, 1)
                        act.wait_ge(xnT_full, b + 1)
                        act.wait_ge(gx_done, b)
                        nc.scalar.activation(xnT[:, :], bk_x[:, :], ACT.Copy).then_inc(xnT_done, 1)
                        act.wait_ge(top_done, b + 1)
                        act.wait_ge(exp1_done, b)
                        nc.scalar.activation(ex[:, :], top[:, :, 0], ACT.Exp, scale=-1.0).then_inc(exp_done, 1)
                        act.wait_ge(oneT_full, b + 1)
                        act.wait_ge(b2_full, b)
                        nc.scalar.activation(oneT[:, :], bk_o[0:EXPERTS, :], ACT.Copy).then_inc(oneT_done, 1)

                @block.vector
                def _(dve):
                    with dve.Fori(0, B) as b:
                        zc = cols(zv, b * SEQ, SEQ)
                        apart(dve)
                        for t in range(TILES):
                            last = nc.vector.bn_stats(st[:, t, :], cols(xv, b * SEQ + t * P, P))
                        last.then_inc(st_done, 1)
                        dve.wait_ge(st_done, b + 1)
                        apart(dve)
                        for t in range(TILES):
                            last = nc.vector.bn_aggr(mv[:, t, :], st[:, t, :])
                        last.then_inc(stats, 1)
                        dve.wait_ge(rstd, b + 1)
                        dve.wait_ge(stats, b + 1)
                        for t in range(TILES):
                            last = nc.vector.tensor_scalar(zb[:, t, :], cols(xv, b * SEQ + t * P, P), mv[:, t, 0:1],
                                                           rs[:, t:t + 1], ALU.subtract, ALU.mult)
                        last.then_inc(z_done, 1)
                        dve.wait_ge(z_done, b + 1)
                        nc.vector.tensor_copy(zc, zb[:, :, :].rearrange("p t d -> p (t d)"))
                        apart(dve)
                        for t in range(TILES):
                            last = nc.vector.bn_stats(st2[:, t, :], zb[:, t, :])
                        last.then_inc(st2_done, 1)
                        dve.wait_ge(st2_done, b + 1)
                        apart(dve)
                        for t in range(TILES):
                            last = nc.vector.bn_aggr(mv2[:, t, :], st2[:, t, :])
                        last.then_inc(stats2, 1)
                        dve.wait_ge(rstd2, b + 1)
                        dve.wait_ge(stats2, b + 1)
                        for t in range(TILES):
                            last = nc.vector.tensor_scalar(xn[:, t, :], zb[:, t, :], mv2[:, t, 0:1],
                                                           rs2[:, t:t + 1], ALU.subtract, ALU.mult)
                        last.then_inc(xn_done, 1)
                        dve.wait_ge(aff_done, b + 1)
                        dve.wait_ge(exp_done, b)
                        apart(dve)
                        for t in range(TILES):
                            last = nc.vector.max(top[:, t, :], aff[:, t, :])
                        last.then_inc(top_done, 1)
                        dve.wait_ge(top_done, b + 1)
                        apart(dve)
                        for t in range(TILES):
                            last = nc.vector.max_index(pick[:, t, :], top[:, t, :], aff[:, t, :])
                        last.then_inc(pick_done, 1)
                        dve.wait_ge(pick_done, b + 1)
                        nc.vector.tensor_copy(pickf[:, :], pick[:, :, 0]).then_inc(pickf_done, 1)
                        dve.wait_ge(pickf_done, b + 1)
                        for t in range(TILES):
                            last = nc.vector.tensor_scalar(oneb[:, t, :], const[:, C_IOTA:C_IOTA + EXPERTS], pickf[:, t:t + 1],
                                                           None, ALU.is_equal)
                        last.then_inc(one_done, 1)
                        dve.wait_ge(one_done, b + 1)
                        nc.vector.tensor_copy(split(cols(one, b * TILES * EXPERTS, TILES * EXPERTS), EXPERTS), oneb[:, :, :])
                        dve.wait_ge(exp_done, b + 1)
                        nc.vector.tensor_scalar(ex1[:, :], ex[:, :], 1.0, None, ALU.add).then_inc(exp1_done, 1)
                        dve.wait_ge(exp1_done, b + 1)
                        nc.vector.reciprocal(cols(alpha, b * TILES, TILES), ex1[:, :]).then_inc(alpha_done, 1)
                        dve.wait_ge(g_full, b + 1)
                        dve.wait_ge(xnT_done, b + 1)
                        dve.wait_ge(xl_done, b)
                        nc.vector.tensor_tensor(gx[:, :], bk_g[:, :], xnT[:, :], ALU.mult).then_inc(gx_done, 1)
                        dve.wait_ge(gx_done, b + 1)
                        nc.vector.tensor_tensor(cols(xl, b * SEQ, SEQ), bk_b[:, :], gx[:, :], ALU.add).then_inc(xl_done, 1)
                        dve.wait_ge(b2_full, b + 1)
                        nc.vector.tensor_copy(cols(acc, b * SEQ, SEQ), bk_y[:, :]).then_inc(acc_done, 1)

                @block.tensor
                def _(pe):
                    pe.wait_ge(w_in, 80)
                    nc.tensor.transpose(bk_a[:, 0:EXPERTS], cen[:, :], ident[0:EXPERTS, 0:EXPERTS]).then_inc(cen_full, 1)
                    pe.wait_ge(cen_done, 1)
                    with pe.Fori(0, B) as b:
                        pe.wait_ge(z_done, b + 1)
                        pe.wait_ge(zT_done, b)
                        for t in range(TILES):
                            last = nc.tensor.transpose(bk_z[:, t * P:(t + 1) * P], zb[:, t, :], ident)
                        last.then_inc(zT_full, 1)
                        pe.wait_ge(zT_done, b + 1)
                        pe.wait_ge(aff_done, b)
                        for t in range(TILES):
                            last = nc.tensor.matmul(bk_a[:, t * EXPERTS:(t + 1) * EXPERTS], zT[:, t * P:(t + 1) * P], cenT[:, :],
                                                    start=True, stop=True)
                        last.then_inc(aff_full, 1)
                        pe.wait_ge(xn_done, b + 1)
                        pe.wait_ge(xnT_done, b)
                        for t in range(TILES):
                            last = nc.tensor.transpose(bk_x[:, t * P:(t + 1) * P], xn[:, t, :], ident)
                        last.then_inc(xnT_full, 1)
                        pe.wait_ge(one_done, b + 1)
                        pe.wait_ge(oneT_done, b)
                        for t in range(TILES):
                            last = nc.tensor.matmul(bk_o[0:EXPERTS, t * P:(t + 1) * P], oneb[:, t, :], ident, start=True, stop=True)
                        last.then_inc(oneT_full, 1)
                        pe.wait_ge(oneT_done, b + 1)
                        pe.wait_ge(xl_done, b)
                        nc.tensor.matmul(bk_g[:, :], gb[:, :], oneT[:, :], start=True, stop=True)
                        nc.tensor.matmul(bk_b[:, :], bb[:, :], oneT[:, :], start=True, stop=True).then_inc(g_full, 1)
                        pe.wait_ge(acc_done, b)
                        for t in range(TILES):
                            last = nc.tensor.matmul(bk_y[:, t * P:(t + 1) * P], oneT[:, t * P:(t + 1) * P], b2s[:, :],
                                                    start=True, stop=True)
                        last.then_inc(b2_full, 1)

        with ExitStack() as banks:
            mb = Memory(nc, banks, "d2")
            bk_h = [mb.bank(f"h{n}") for n in range(4)]
            bk_y = [mb.bank(f"y{n}") for n in range(2)]
            with nc.Block() as block:
                @block.sync
                def _(sp):
                    def load(e, s):
                        sp.dma_start(w1s[:, s, :], w1[bass.ds(e, 1), :, :].rearrange("o p n -> (o p) n")).then_inc(e_in[s], 16)
                        sp.dma_start(w2s[:, s, :, :], w2[bass.ds(e, 1), :, :].rearrange("o (f p) n -> (o p) f n", p=P)).then_inc(e_in[s], 16)

                    for s in range(2):
                        load(s, s)
                    with sp.Fori(1, EXPERTS // 2) as i:
                        for s in range(2):
                            sp.wait_ge(y_full, (i * 2 + s - 1) * B)
                            load(i * 2 + s, s)
                    for b in range(B):
                        sp.wait_ge(out_done, b + 1)
                        sp.dma_start(out_h[b, :, :].rearrange("(t p) d -> p t d", p=P),
                                     split(X[:, b * SEQ:(b + 1) * SEQ], P)).then_inc(stored, 16)
                    sp.wait_ge(stored, 16 * B)

                @block.scalar
                def _(act):
                    with act.Fori(0, EXPERTS // 2) as i:
                        for s in range(2):
                            for b in range(B):
                                n = (i * 2 + s) * B + b
                                for f in range(FCH):
                                    act.wait_ge(h_full, n * FCH + f + 1)
                                    if f == 0 and (s or b >= 2):
                                        act.wait_ge(y_full, n - 1)
                                    elif f == 0:
                                        act.wait_ge(y_full, i * 2 * B + b - (1 if b else 0))
                                    apart(act)
                                    nc.scalar.activation(hT[:, b % 2, f, :], bk_h[f][:, :], ACT.Relu,
                                                         bias=cols(b1c, (i * 2 + s) * FCH + f, 1)).then_inc(h_done, 1)

                @block.vector
                def _(dve):
                    with dve.Fori(0, EXPERTS // 2) as i:
                        for s in range(2):
                            for b in range(B):
                                n = (i * 2 + s) * B + b
                                dve.wait_ge(y_full, n + 1)
                                dve.wait_ge(y_done, i * 2 * B + (s * B))
                                for t in range(TILES):
                                    at = (b * TILES + t) * P
                                    mine = cols(one, (b * TILES + t) * EXPERTS + i * 2 + s, 1)
                                    last = nc.vector.scalar_tensor_tensor(acc[:, at:at + P], bk_y[b % 2][:, t * P:(t + 1) * P],
                                                                          mine, acc[:, at:at + P], ALU.mult, ALU.add)
                                last.then_inc(y_done, 1)
                    for b in range(B):
                        dve.wait_ge(y_done, (EXPERTS - 1) * B + b + 1)
                        for t in range(TILES):
                            u = b * TILES + t
                            last = nc.vector.scalar_tensor_tensor(fin[:, u * P:(u + 1) * P], acc[:, u * P:(u + 1) * P],
                                                                  alpha[:, u:u + 1], XS[:, u * P:(u + 1) * P], ALU.mult, ALU.add)
                        last.then_inc(gated_done, 1)
                        dve.wait_ge(gated_done, b + 1)
                        at = slice(b * SEQ, (b + 1) * SEQ)
                        nc.vector.tensor_tensor(X[:, at], X[:, at], fin[:, at], ALU.add).then_inc(out_done, 1)

                @block.tensor
                def _(pe):
                    with pe.Fori(0, EXPERTS // 2) as i:
                        def hidden(s, b):
                            n = (i * 2 + s) * B + b
                            if b == 0:
                                pe.wait_ge(e_in[s], i * 32 + 32)
                            for f in range(FCH):
                                if s or b:
                                    pe.wait_ge(h_done, (n - 1) * FCH + f + 1)
                                else:
                                    pe.wait_ge(h_done, i * 2 * B * FCH)
                                nc.tensor.matmul(bk_h[f][:, :], w1s[:, s, f * P:(f + 1) * P], xl[:, b * SEQ:(b + 1) * SEQ],
                                                 start=True, stop=True).then_inc(h_full, 1)

                        groups = [(s, b) for s in range(2) for b in range(B)]
                        hidden(*groups[0])
                        for g, (s, b) in enumerate(groups):
                            n = i * 2 * B + g
                            if g + 1 < len(groups):
                                hidden(*groups[g + 1])
                            pe.wait_ge(h_done, (n + 1) * FCH)
                            pe.wait_ge(y_done, n - 1 if g else i * 2 * B)
                            for t in range(TILES):
                                for f in range(FCH):
                                    last = nc.tensor.matmul(bk_y[b % 2][:, t * P:(t + 1) * P],
                                                            hT[:, b % 2, f, t * P:(t + 1) * P], w2s[:, s, f, :],
                                                            start=(f == 0), stop=(f == FCH - 1))
                            last.then_inc(y_full, 1)


def program(nc, a, out_h):
    with ExitStack() as es:
        X = es.enter_context(nc.sbuf_tensor("residual", [P, NT * P], fp32))
        XS = es.enter_context(nc.sbuf_tensor("stream", [P, NT * P], fp32))
        const = es.enter_context(nc.sbuf_tensor("const_tables", [P, C_ALL], fp32))
        cross_attention(nc, const, X, XS, a["ctx_1024"], a["L0_xattn_w_sim"], a["L0_xattn_b_sim"], a["L0_xattn_W_qv"],
                        a["L0_xattn_b_qv"], a["x"], a["constants"])
        windowed_layers(nc, const, XS, *[a["L0_ffn_" + n] for n in
                                         ("Wqkv", "q_scale", "k_scale", "Wo", "ln_g", "ln_b", "W1", "b1", "W2", "b2")])
        gathered_attention(nc, const, X, XS, a["ctx_1024"], a["L1_xattn_Wq"], a["L1_xattn_Wkv"], a["L1_xattn_Wc"])
        mixture(nc, const, X, XS, *[a["L1_ffn_" + n] for n in
                                    ("centroids", "ln_g", "ln_b", "w1", "b1", "w2", "b2")], out_h)


INPUTS = ["x", "ctx_1024", "L0_xattn_w_sim", "L0_xattn_b_sim", "L0_xattn_W_qv", "L0_xattn_b_qv", "L0_ffn_Wqkv",
          "L0_ffn_q_scale", "L0_ffn_k_scale", "L0_ffn_Wo", "L0_ffn_ln_g", "L0_ffn_ln_b", "L0_ffn_W1", "L0_ffn_b1",
          "L0_ffn_W2", "L0_ffn_b2", "L1_xattn_Wq", "L1_xattn_Wkv", "L1_xattn_Wc", "L1_ffn_centroids", "L1_ffn_ln_g",
          "L1_ffn_ln_b", "L1_ffn_w1", "L1_ffn_b1", "L1_ffn_w2", "L1_ffn_b2"]


def kernel(**inputs):
    from concourse import bacc
    from concourse.bass_utils import run_bass_kernel_spmd

    nc = bacc.Bacc("TRN2", target_bir_lowering=False, num_devices=1)
    arrays = {n: np.ascontiguousarray(inputs[n]) for n in INPUTS}
    arrays["constants"] = constants()
    aps = {n: nc.dram_tensor(n, v.shape, mybir.dt.from_np(v.dtype), kind="ExternalInput").ap() for n, v in arrays.items()}
    out = nc.dram_tensor("out", (B, SEQ, P), fp32, kind="ExternalOutput").ap()
    program(nc, aps, out)
    r = run_bass_kernel_spmd(nc, [arrays], core_ids=[0])
    return r.results[0]["out"]
```
